# Optimizing a Trainium2 kernel written in Bass

```python
import numpy as np
import jax
import jax.numpy as jnp

def _softmax(x, axis=-1):
    return jax.nn.softmax(x, axis=axis)

def _gelu(x):
    return jax.nn.gelu(x, approximate=True)

def _silu(x):
    return jax.nn.silu(x)

def _sigmoid(x):
    return jax.nn.sigmoid(x)

def _layernorm(x, axis=-1, eps=1e-05):
    m = jnp.mean(x, axis=axis, keepdims=True)
    v = jnp.var(x, axis=axis, keepdims=True)
    return (x - m) / jnp.sqrt(v + eps)

def _scatter_add(tgt, idx, src, axis=0):
    return tgt.at[idx].add(src)

def _segment_sum(src, seg, n):
    return jax.ops.segment_sum(src, seg, n)
kernel_name = 'mk_gnn_resnorm_d1_gnn_r32_7e2069'

def setup_inputs(seed: int=0):
    np.random.seed(seed)
    _w = jnp.asarray

    def _rec_inputs():
        import jax
        import jax.numpy as jnp
        _gk = jax.random.key(seed)
        x = -1.785e-05 + 0.08841 * jax.random.normal(jax.random.fold_in(_gk, 1), (50000, 128), jnp.float32)
        src = jax.random.randint(jax.random.fold_in(_gk, 2), (25000,), 0, 50000, jnp.int32)
        dst = jnp.minimum((50000 * jax.random.uniform(jax.random.fold_in(_gk, 3), (25000,)) ** 2.0).astype(jnp.int32), 49999)
        _o = jnp.argsort(dst, stable=True)
        src = src[_o]
        dst = dst[_o]
        edge_type_16 = jax.random.randint(jax.random.fold_in(_gk, 12), (25000,), 0, 16, jnp.int32)
        return (x, src, dst, edge_type_16)
    x, src, dst, edge_type_16 = _rec_inputs()

    def _L0_gnn_setup():
        import jax, jax.numpy as jnp
        import numpy as np
        N_ENT = 50000
        N_REL = 16
        N_BASES = 8
        H_DIM = 128
        N_EDGES = 25000

        def _rgcn_layer(h, src, dst, rel, basis, w_comp, loop_w, bias):
            W = jnp.einsum('rb,bio->rio', w_comp, basis)
            seg = dst.astype(jnp.int32) * N_REL + rel.astype(jnp.int32)
            agg = jax.ops.segment_sum(h[src], seg, num_segments=N_ENT * N_REL)
            agg = agg.reshape(N_ENT, N_REL, -1)
            msg = jnp.einsum('nri,rio->no', agg, W)
            out = msg + h @ loop_w + bias
            return jax.nn.relu(out)
        key = jax.random.key(seed)
        ks = jax.random.split(key, 12)
        s = 1.0 / np.sqrt(H_DIM)
        inp = {'entity_emb': jax.random.normal(ks[0], (N_ENT, H_DIM), jnp.float32) * s, 'basis1': jax.random.normal(ks[1], (N_BASES, H_DIM, H_DIM), jnp.float32) * s, 'w_comp1': jax.random.normal(ks[2], (N_REL, N_BASES), jnp.float32) * (1.0 / np.sqrt(N_BASES)), 'loop_w1': jax.random.normal(ks[3], (H_DIM, H_DIM), jnp.float32) * s, 'bias1': jnp.zeros((H_DIM,), jnp.float32), 'basis2': jax.random.normal(ks[4], (N_BASES, H_DIM, H_DIM), jnp.float32) * s, 'w_comp2': jax.random.normal(ks[5], (N_REL, N_BASES), jnp.float32) * (1.0 / np.sqrt(N_BASES)), 'loop_w2': jax.random.normal(ks[6], (H_DIM, H_DIM), jnp.float32) * s, 'bias2': jnp.zeros((H_DIM,), jnp.float32), 'src': jax.random.randint(ks[7], (N_EDGES,), 0, N_ENT, jnp.int32), 'dst': jax.random.randint(ks[8], (N_EDGES,), 0, N_ENT, jnp.int32), 'rel_type': jax.random.randint(ks[9], (N_EDGES,), 0, N_REL, jnp.int32)}
        return inp
    _L0_gnn_all = _L0_gnn_setup()
    _L0_gnn_in = {k: v for k, v in _L0_gnn_all.items() if k in ('basis1', 'w_comp1', 'loop_w1', 'bias1', 'basis2', 'w_comp2', 'loop_w2', 'bias2')}
    del _L0_gnn_all
    return {'x': x, 'src': src, 'dst': dst, 'edge_type_16': edge_type_16, 'L0_gnn_basis1': _L0_gnn_in['basis1'], 'L0_gnn_w_comp1': _L0_gnn_in['w_comp1'], 'L0_gnn_loop_w1': _L0_gnn_in['loop_w1'], 'L0_gnn_bias1': _L0_gnn_in['bias1'], 'L0_gnn_basis2': _L0_gnn_in['basis2'], 'L0_gnn_w_comp2': _L0_gnn_in['w_comp2'], 'L0_gnn_loop_w2': _L0_gnn_in['loop_w2'], 'L0_gnn_bias2': _L0_gnn_in['bias2']}

def reference(x, src, dst, edge_type_16, L0_gnn_basis1, L0_gnn_w_comp1, L0_gnn_loop_w1, L0_gnn_bias1, L0_gnn_basis2, L0_gnn_w_comp2, L0_gnn_loop_w2, L0_gnn_bias2):
    import jax
    import jax.numpy as jnp

    def _L0_gnn_ref(entity_emb, basis1, w_comp1, loop_w1, bias1, basis2, w_comp2, loop_w2, bias2, src, dst, rel_type):
        import jax, jax.numpy as jnp
        import numpy as np
        N_ENT = 50000
        N_REL = 16
        N_BASES = 8
        H_DIM = 128
        N_EDGES = 25000

        def _rgcn_layer(h, src, dst, rel, basis, w_comp, loop_w, bias):
            W = jnp.einsum('rb,bio->rio', w_comp, basis)
            seg = dst.astype(jnp.int32) * N_REL + rel.astype(jnp.int32)
            agg = jax.ops.segment_sum(h[src], seg, num_segments=N_ENT * N_REL)
            agg = agg.reshape(N_ENT, N_REL, -1)
            msg = jnp.einsum('nri,rio->no', agg, W)
            out = msg + h @ loop_w + bias
            return jax.nn.relu(out)
        h = _rgcn_layer(entity_emb, src, dst, rel_type, basis1, w_comp1, loop_w1, bias1)
        h = _rgcn_layer(h, src, dst, rel_type, basis2, w_comp2, loop_w2, bias2)
        return h
    x = _layernorm(x + _L0_gnn_ref(x, L0_gnn_basis1, L0_gnn_w_comp1, L0_gnn_loop_w1, L0_gnn_bias1, L0_gnn_basis2, L0_gnn_w_comp2, L0_gnn_loop_w2, L0_gnn_bias2, src, dst, edge_type_16), axis=-1)
    return x

_drawn_inputs = setup_inputs


def setup_inputs(seed=0):
    import zlib

    import numpy as np

    out = dict(_drawn_inputs(seed))
    spreads = {'L0_gnn_bias1': (0.0, 0.1), 'L0_gnn_bias2': (0.0, 0.1)}
    factors = {}
    for name, (base, spread) in spreads.items():
        noise = np.random.default_rng([zlib.crc32(name.encode()), seed]).standard_normal(out[name].shape)
        drawn = base * np.exp(spread * noise) if base else spread * noise
        out[name] = jnp.asarray(drawn.astype(out[name].dtype))
    for name, factor in factors.items():
        out[name] = (out[name] * factor).astype(out[name].dtype)
    return out
```

```python
from contextlib import ExitStack

import concourse.bass as bass
from concourse import mybir

F32 = mybir.dt.float32
BF16 = mybir.dt.bfloat16
I32 = mybir.dt.int32
ALU = mybir.AluOpType
ACT = mybir.ActivationFunctionType
AX = mybir.AxisListType

P = 128
N = 50000
E = 25000
D = 128
NREL = 16
NB = 8

CH = -(-E // P)
U = 4
TURNS = CH // U
FULL = E // P
REST = E - FULL * P
HALF1 = FULL - P

J = 8
Q = 4
BLK = J * P
NBLK = N // BLK
TAILQ = (N - NBLK * BLK) // P
TAIL = N - NBLK * BLK - TAILQ * P
NBUF = 2
DTURNS = NBLK // U
HALVES = 2 * NBLK + 2

SC = 14
DUMMY = N
ROWS = DUMMY + SC * P

FJ = 10
FBLK = FJ * P
FN = N // FBLK
FBUF = 3
EPS = 1e-5


def build_rgcn(nc, x, src, dst, rel, basis1, w_comp1, loop_w1, bias1,
               basis2, w_comp2, loop_w2, bias2, out):
    ctx = ExitStack()
    with ctx:
        def sb(name, shape, dt=F32):
            return ctx.enter_context(nc.sbuf_tensor(name, shape, dt))

        def ps(name, shape):
            return ctx.enter_context(nc.psum_tensor(name, shape, F32))

        def sem(name):
            return ctx.enter_context(nc.semaphore(name))

        nodes = [nc.dram_tensor(f"nodes{l}", (ROWS, D), F32).ap() for l in range(2)]
        same_d = nc.dram_tensor("same_d", (CH * P,), BF16).ap()

        sums = sb("sums", [P, CH, D])
        same = sb("same", [P, CH * P], BF16)
        coef = [sb(f"coef{l}", [P, CH, NB]) for l in range(2)]
        src_i = sb("src_i", [P, CH], I32)
        put_i = sb("put_i", [P, CH], I32)
        dst_f = sb("dst_f", [P, CH])
        last_f = sb("last_f", [P, CH])
        rel_f = sb("rel_f", [P, CH])
        basis = [sb(f"basis{l}", [P, NB, D]) for l in range(2)]
        loop_w = [sb(f"loop_w{l}", [P, D]) for l in range(2)]
        ident = sb("ident", [P, P])
        bias1_c = sb("bias1_c", [P, 1])
        bias2_b = sb("bias2_b", [P, D])
        w_b = [sb(f"w_b{l}", [P, NREL * NB]) for l in range(2)]
        rel_no = sb("rel_no", [P, NREL])
        unsorted_i = sb("unsorted_i", [1, 1], I32)
        xin = sb("xin", [P, NBUF, J, D])
        yout = sb("yout", [P, NBUF, J, D])
        stage = sb("stage", [P, 2, D])
        gT = sb("gT", [P, 2, P])
        msg = sb("msg", [P, 2, D])
        run = sb("run", [P, 2, P])
        xT = sb("xT", [P, 2, Q * P])

        def scratch(first, chunks):
            return sums[:, first:first + chunks, :]
        raw = {k: scratch(CH - 20 + 2 * i, 2).bitcast(I32) for i, k in enumerate(("src", "dst", "nxt", "prv", "rel"))}
        val = {k: scratch(CH - 10 + 2 * i, 2) for i, k in enumerate(("src", "dst", "last", "rel"))}
        bigger = scratch(CH - 2, 2)
        dummy_i = sums[:, CH - 22:CH - 20, :].rearrange("p a d -> p (a d)")[:, 0:CH].bitcast(I32)
        away = sums[:, CH - 24:CH - 22, :].rearrange("p a d -> p (a d)")[:, 0:CH]
        same_h = sums[:, CH - 25, :].bitcast(BF16).rearrange("p (a d) -> p a d", a=2)
        zeros = scratch(CH - 39, SC)
        eq = [scratch(CH - 45, 4).rearrange("p (s a) d -> p s (a d)", s=2)[:, :, 0:CH],
              yout[:, :, :, :].rearrange("p s j d -> p s (j d)")[:, :, 0:CH]]
        rel_no_i = sums[:, CH - 46, 32:32 + NREL].bitcast(I32)
        ones_c = sums[:, CH - 46, 64:65]
        worst = sums[:, CH - 46, 65:66]

        ps_g = ps("ps_g", [P, 4, P])
        ps_m = ps("ps_m", [P, 4, P])
        ps_x = ps("ps_x", [P, Q * P])
        ps_y = ps("ps_y", [P, Q * D])
        ps_b = [ps(f"ps_b{s}", [P, NB, D]) for s in range(2)]

        cleared = sem("cleared")
        idx_in = sem("idx_in")
        weights_in = sem("weights_in")
        ident_ok = sem("ident_ok")
        iota_ok = sem("iota_ok")
        vdone = sem("vdone")
        setup_t = sem("setup_t")
        idx_ok = sem("idx_ok")
        coef_ok = sem("coef_ok")
        same_w = sem("same_w")
        same_in = sem("same_in")
        zero_w = sem("zero_w")
        gathered = [sem(f"gathered{u}") for u in range(U)]
        staged = sem("staged")
        gt_made = sem("gt_made")
        gt_moved = sem("gt_moved")
        based = sem("based")
        msg_made = sem("msg_made")
        msg_t = sem("msg_t")
        scanned = sem("scanned")
        run_t = sem("run_t")
        summed = sem("summed")
        linked = sem("linked")
        halved = sem("halved")
        x_in = [sem(f"x_in{b}") for b in range(NBUF)]
        xt_made = sem("xt_made")
        xt_moved = sem("xt_moved")
        y_made = sem("y_made")
        y_moved = sem("y_moved")
        y_out = [sem(f"y_out{b}") for b in range(NBUF)]
        put = [sem(f"put{u}") for u in range(SC)]
        f_in = [sem(f"f_in{b}") for b in range(FBUF)]
        f_sum = sem("f_sum")
        f_stat = sem("f_stat")
        f_var = sem("f_var")
        f_std = sem("f_std")
        f_norm = sem("f_norm")
        f_done = sem("f_done")
        f_out = [sem(f"f_out{b}") for b in range(FBUF)]


        def y_total(b, l):
            return 16 * (NBLK // NBUF + 2 * (b == 0)) * (l + 1)

        def put_total(u, l):
            return 16 * (l + 1) * (CH // SC)

        def node_block(k, l):
            t = x if l == 0 else nodes[0]
            return t[bass.ds(k * BLK, BLK), :].rearrange("(p j) d -> p j d", j=J)

        def wait(eng, s, v):
            if not isinstance(v, int) or v > 0:
                eng.wait_ge(s, v)

        def final_tiles(b):
            h = sums[:, 20 * b:20 * b + FJ, :]
            xx = sums[:, 20 * b + FJ:20 * b + 2 * FJ, :]
            return h, xx

        def last_load(sp):
            def load(k, b):
                h, xx = final_tiles(b)
                sp.dma_start(h, nodes[1][bass.ds(k * FBLK, FBLK), :].rearrange("(p j) d -> p j d", j=FJ)).then_inc(f_in[b], 16)
                sp.dma_start(xx, x[bass.ds(k * FBLK, FBLK), :].rearrange("(p j) d -> p j d", j=FJ)).then_inc(f_in[b], 16)

            def store(k, b):
                h, xx = final_tiles(b)
                sp.wait_ge(f_done, k + 1)
                sp.dma_start(out[bass.ds(k * FBLK, FBLK), :].rearrange("(p j) d -> p j d", j=FJ), xx).then_inc(f_out[b], 16)

            for b in range(FBUF):
                load(b, b)
            with sp.Fori(0, FN // FBUF - 1) as r:
                for b in range(FBUF):
                    store(r * FBUF + b, b)
                    sp.wait_ge(f_out[b], r * 16 + 16)
                    load(r * FBUF + (b + FBUF), b)
            for b in range(FBUF):
                store(FN - FBUF + b, b)
            h, xx = final_tiles(0)
            sp.wait_ge(f_out[0], 16 * (FN // FBUF))
            sp.dma_start(h[0:TAIL, 0, :], nodes[1][N - TAIL:N, :]).then_inc(f_in[0], 16)
            sp.dma_start(xx[0:TAIL, 0, :], x[N - TAIL:N, :]).then_inc(f_in[0], 16)
            sp.wait_ge(f_done, FN + 1)
            sp.dma_start(out[N - TAIL:N, :], xx[0:TAIL, 0, :]).then_inc(f_out[0], 16)
            for b in range(FBUF):
                sp.wait_ge(f_out[b], 16 * (FN // FBUF + (b == 0)))

        def stage_stats(dve):
            small = sums[:, 100, :]
            return {
                "bn": [sums[:, 102 + b, 0:6 * FJ].rearrange("p (j s) -> p j s", s=6) for b in range(FBUF)],
                "s": [sums[:, 106 + b, 0:FJ] for b in range(FBUF)],
                "d": [sums[:, 106 + b, 16:16 + FJ] for b in range(FBUF)],
                "q": [sums[:, 106 + b, 32:32 + FJ] for b in range(FBUF)],
                "v": [sums[:, 106 + b, 48:48 + FJ] for b in range(FBUF)],
                "r": [sums[:, 106 + b, 64:64 + FJ] for b in range(FBUF)],
                "o": [sums[:, 106 + b, 80:80 + FJ] for b in range(FBUF)],
            }

        def last_vector(dve, f):
            def add_rows(k, b, rows, nj, turn):
                h, xx = final_tiles(b)
                dve.wait_ge(f_in[b], turn * 32 + 32)
                hv, xv = (a[0:rows, 0:nj, :].rearrange("p j d -> p (j d)") for a in (h, xx))
                nc.vector.scalar_tensor_tensor(out=hv, in0=hv, scalar=0.0, in1=xv,
                                               op0=ALU.max, op1=ALU.add).then_inc(f_sum, 1)
                dve.wait_ge(f_sum, k + 1)
                for j in range(nj):
                    i = nc.vector.bn_stats(f["bn"][b][0:rows, j, :], h[0:rows, j, :])
                i.then_inc(f_stat, 1)

            def var(k, b, rows, nj):
                g = {n: f[n][b][0:rows, 0:nj] for n in "sdqvro"}
                bn = f["bn"][b][0:rows, 0:nj, :]
                dve.wait_ge(f_stat, k + 1)
                nc.vector.tensor_tensor(g["s"], bn[:, :, 1], bn[:, :, 4], ALU.add)
                nc.vector.tensor_tensor(g["d"], bn[:, :, 1], bn[:, :, 4], ALU.subtract)
                nc.vector.tensor_tensor(g["q"], bn[:, :, 2], bn[:, :, 5], ALU.add).then_inc(f_var, 1)
                dve.wait_ge(f_var, k * 4 + 1)
                nc.vector.tensor_tensor(g["d"], g["d"], g["d"], ALU.mult)
                nc.vector.tensor_scalar(g["q"], g["q"], 1.0 / D, EPS, ALU.mult, ALU.add).then_inc(f_var, 1)
                dve.wait_ge(f_var, k * 4 + 2)
                nc.vector.scalar_tensor_tensor(out=g["v"], in0=g["d"], scalar=0.25, in1=g["q"],
                                               op0=ALU.mult, op1=ALU.add).then_inc(f_var, 1)

            def scale(k, b, rows, nj):
                g = {n: f[n][b][0:rows, 0:nj] for n in "sdqvro"}
                dve.wait_ge(f_std, k + 1)
                nc.vector.reciprocal(g["r"], g["q"]).then_inc(f_var, 1)
                dve.wait_ge(f_var, k * 4 + 4)
                nc.vector.scalar_tensor_tensor(out=g["o"], in0=g["s"], scalar=-0.5, in1=g["r"],
                                               op0=ALU.mult, op1=ALU.mult).then_inc(f_norm, 1)

            def one(k, b, turn, rows=P, nj=FJ):
                add_rows(k, b, rows, nj, turn)
                var(k, b, rows, nj)
                scale(k, b, rows, nj)

            with dve.Fori(0, FN // FBUF) as r:
                for b in range(FBUF):
                    one(r * FBUF + b, b, r)
            one(FN, 0, FN // FBUF, TAIL, 1)

        block = ctx.enter_context(nc.Block())

        @block.sync
        def _(sp):
            def load_edges(tile, a, shift):
                cut = P * P + shift
                if shift < 0:
                    sp.dma_start(tile[0:1, 0, 1:P], a[0:P - 1].rearrange("(p j) -> p j", p=1)).then_inc(idx_in, 16)
                    sp.dma_start(tile[1:P, 0, :], a[P - 1:cut].rearrange("(p j) -> p j", j=P)).then_inc(idx_in, 16)
                else:
                    sp.dma_start(tile[:, 0, :], a[shift:cut].rearrange("(p j) -> p j", j=P)).then_inc(idx_in, 16)
                end = cut + HALF1 * P
                left = min(REST, E - end)
                sp.dma_start(tile[0:HALF1, 1, :], a[cut:end].rearrange("(p j) -> p j", j=P)).then_inc(idx_in, 16)
                sp.dma_start(tile[HALF1:HALF1 + 1, 1, 0:left],
                             a[end:end + left].rearrange("(p j) -> p j", p=1)).then_inc(idx_in, 16)

            sp.wait_ge(cleared, 1)
            load_edges(raw["src"], src, 0)
            load_edges(raw["dst"], dst, 0)
            load_edges(raw["nxt"], dst, 1)
            load_edges(raw["prv"], dst, -1)
            load_edges(raw["rel"], rel, 0)

            sp.dma_start(w_b[0][:, :], w_comp1.rearrange("r b -> (r b)").partition_broadcast(P)).then_inc(weights_in, 16)
            sp.dma_start(w_b[1][:, :], w_comp2.rearrange("r b -> (r b)").partition_broadcast(P)).then_inc(weights_in, 16)
            sp.dma_start(basis[0][:, :, :], basis1.rearrange("b i o -> i b o")).then_inc(weights_in, 16)
            sp.dma_start(basis[1][:, :, :], basis2.rearrange("b i o -> i b o")).then_inc(weights_in, 16)
            sp.dma_start(loop_w[0][:, :], loop_w1).then_inc(weights_in, 16)
            sp.dma_start(loop_w[1][:, :], loop_w2).then_inc(weights_in, 16)
            sp.dma_start(bias1_c[:, :], bias1.rearrange("(p a) -> p a", a=1)).then_inc(weights_in, 16)
            sp.dma_start(bias2_b[:, :], bias2.partition_broadcast(P)).then_inc(weights_in, 16)
            for l in range(2):
                sp.dma_start(nodes[l][DUMMY:ROWS, :].rearrange("(s p) d -> p s d", p=P), zeros[:, :, :]).then_inc(zero_w, 16)
            sp.wait_ge(same_w, 1)
            sp.dma_start(same_d[0:P * P].rearrange("(p j) -> p j", j=P), same_h[:, 0, :]).then_inc(same_w, 16)
            sp.dma_start(same_d[P * P:CH * P].rearrange("(p j) -> p j", j=P), same_h[0:CH - P, 1, :]).then_inc(same_w, 16)
            sp.wait_ge(same_w, 33)
            sp.dma_start(same[:, :], same_d.partition_broadcast(P)).then_inc(same_in, 16)

            for l in range(2):
                if l == 1:
                    for u in range(SC):
                        sp.wait_ge(put[u], put_total(u, 0))
                for b in range(NBUF):
                    sp.dma_start(xin[:, b, :, :], node_block(b, l)).then_inc(x_in[b], 16)
                h0 = l * HALVES

                def move_block(k, b, more):
                    if more:
                        sp.wait_ge(xt_made, k * 2 + (h0 + 2))
                        sp.dma_start(xin[:, b, :, :], node_block(k + NBUF, l)).then_inc(x_in[b], 16)
                    sp.wait_ge(y_moved, k * 2 + (h0 + 2))
                    sp.dma_start(nodes[l][bass.ds(k * BLK, BLK), :].rearrange("(p j) d -> p j d", j=J),
                                 yout[:, b, :, :]).then_inc(y_out[b], 16)

                with sp.Fori(0, NBLK // NBUF - 1) as r:
                    for b in range(NBUF):
                        move_block(r * NBUF + b, b, True)
                t = x if l == 0 else nodes[0]
                lo = NBLK * BLK
                mid = lo + TAILQ * P
                sp.wait_ge(xt_made, h0 + 2 * (NBLK - 1))
                sp.dma_start(xin[:, 0, 0:TAILQ, :], t[lo:mid, :].rearrange("(p j) d -> p j d", j=TAILQ)).then_inc(x_in[0], 16)
                sp.dma_start(xin[0:TAIL, 0, TAILQ, :], t[mid:N, :]).then_inc(x_in[0], 16)
                for b in range(NBUF):
                    move_block(NBLK - NBUF + b, b, False)
                sp.wait_ge(y_moved, h0 + HALVES)
                sp.dma_start(nodes[l][lo:mid, :].rearrange("(p j) d -> p j d", j=TAILQ),
                             yout[:, 0, 0:TAILQ, :]).then_inc(y_out[0], 16)
                sp.dma_start(nodes[l][mid:N, :], yout[0:TAIL, 0, TAILQ, :]).then_inc(y_out[0], 16)

            for u in range(SC):
                sp.wait_ge(put[u], put_total(u, 1))
            last_load(sp)

        @block.gpsimd
        def _(pool):
            limit = pool.snap(pool.to_reg(ROWS - 1))
            pool.memset(ident[:, :], 0.0).then_inc(ident_ok, 1)
            pool.wait_ge(ident_ok, 1)
            pool.affine_select(out=ident[:, :], in_=ident[:, :], compare_op=ALU.not_equal, fill=1.0,
                               base=0, pattern=[[-1, P]], channel_multiplier=1).then_inc(ident_ok, 1)
            pool.iota(dummy_i, pattern=[[0, CH // SC], [P, SC]], base=DUMMY, channel_multiplier=1).then_inc(iota_ok, 1)
            pool.iota(rel_no_i, pattern=[[1, NREL]], base=0, channel_multiplier=0).then_inc(iota_ok, 1)
            pool.wait_ge(idx_ok, 1)
            flag = pool.value_load(unsorted_i[0:1, 0:1], min_val=0, max_val=E)

            def scatter(l, c):
                pool.wait_ge(summed, l * CH + c + 1)
                if l * CH + c >= SC:
                    pool.wait_ge(put[c % SC], 16 * (l * (CH // SC) + c // SC))
                pool.indirect_dma_start(
                    out=nodes[l][:, :], out_offset=bass.IndirectOffsetOnAxis(ap=put_i[:, c:c + 1], axis=0),
                    in_=sums[:, c, :], in_offset=None, bounds_check=limit, oob_is_err=True,
                    compute_op=ALU.add).then_inc(put[c % SC], 16)

            for l in range(2):
                table = x if l == 0 else nodes[0]
                for c in range(CH):
                    if l == 0 and c == CH - 46:
                        pool.wait_ge(coef_ok, 1)
                        pool.wait_ge(zero_w, 32)
                        pool.wait_ge(same_w, 33)
                        pool.wait_ge(setup_t, 1)
                    if l * CH + c >= U:
                        turn = l * TURNS + c // U
                        pool.wait_ge(gathered[c % U], 16 * turn)
                    pool.indirect_dma_start(
                        out=sums[:, c, :], out_offset=None, in_=table[:, :],
                        in_offset=bass.IndirectOffsetOnAxis(ap=src_i[:, c:c + 1], axis=0)).then_inc(gathered[c % U], 16)
                for b in range(NBUF):
                    pool.wait_ge(y_out[b], y_total(b, l))
                for c in range(CH):
                    scatter(l, c)
                for u in range(SC):
                    pool.wait_ge(put[u], put_total(u, l))

        @block.vector
        def _(dve):
            steps = [0]

            def step(ins):
                steps[0] += 1
                ins.then_inc(vdone, 1)
                dve.wait_ge(vdone, steps[0])

            step(nc.vector.memset(raw["src"], 0))
            step(nc.vector.memset(raw["dst"], DUMMY))
            step(nc.vector.memset(raw["nxt"], DUMMY))
            step(nc.vector.memset(raw["prv"], -1))
            step(nc.vector.memset(zeros, 0.0))
            step(nc.vector.memset(ones_c, 1.0))
            nc.vector.memset(raw["rel"], 0).then_inc(cleared, 1)
            dve.wait_ge(idx_in, 16 * 16)
            step(nc.vector.tensor_copy(val["src"], raw["src"]))
            step(nc.vector.tensor_copy(val["dst"], raw["dst"]))
            step(nc.vector.tensor_copy(val["rel"], raw["rel"]))
            step(nc.vector.tensor_tensor(val["last"], raw["dst"], raw["nxt"], ALU.not_equal))
            nc.vector.tensor_tensor(same_h, raw["dst"], raw["prv"], ALU.is_equal).then_inc(same_w, 1)
            step(nc.vector.tensor_tensor(bigger, raw["dst"], raw["nxt"], ALU.is_gt))
            step(nc.vector.reduce_sum(worst, bigger.rearrange("p a d -> p (a d)"), axis=AX.X))
            dve.wait_ge(setup_t, 1)
            step(nc.vector.tensor_copy(src_i[:, :], ps_b[0][:, 0:4, :].rearrange("p a d -> p (a d)")[:, 0:CH]))
            step(nc.vector.tensor_copy(dst_f[:, :], ps_b[0][:, 4:8, :].rearrange("p a d -> p (a d)")[:, 0:CH]))
            step(nc.vector.tensor_copy(last_f[:, :], ps_b[1][:, 0:4, :].rearrange("p a d -> p (a d)")[:, 0:CH]))
            step(nc.vector.tensor_copy(rel_f[:, :], ps_b[1][:, 4:8, :].rearrange("p a d -> p (a d)")[:, 0:CH]))
            step(nc.vector.tensor_copy(unsorted_i[:, :], ps_m[0:1, 0, 0:1]))
            dve.wait_ge(iota_ok, 2)
            step(nc.vector.tensor_tensor(away, dst_f[:, :], dummy_i, ALU.subtract))
            step(nc.vector.tensor_tensor(away, away, last_f[:, :], ALU.mult))
            step(nc.vector.tensor_tensor(put_i[:, :], away, dummy_i, ALU.add))
            step(nc.vector.tensor_copy(rel_no[:, :], rel_no_i))
            nc.vector.memset(coef[0][:, :, :], 0.0).then_inc(idx_ok, 1)
            dve.wait_ge(weights_in, 16 * 8)

            def coefficients(l):
                for r in range(NREL):
                    step(nc.vector.tensor_scalar(eq[l][:, r % 2, :], rel_f[:, :], rel_no[:, r:r + 1], None, ALU.is_equal))
                    for b in range(NB):
                        i = nc.vector.scalar_tensor_tensor(out=coef[l][:, :, b], in0=eq[l][:, r % 2, :],
                                                           scalar=w_b[l][:, r * NB + b:r * NB + b + 1],
                                                           in1=coef[l][:, :, b], op0=ALU.mult, op1=ALU.add)
                    if r < NREL - 1:
                        step(i)
                    else:
                        i.then_inc(coef_ok, 1)

            dve.wait_ge(idx_ok, 1)
            coefficients(0)
            dve.wait_ge(coef_ok, 1)
            dve.wait_ge(same_in, 16)


            def messages(c, s, l, n, links, half):
                wait(dve, based, n * 2 + (1 + half))
                if half == 0:
                    wait(dve, msg_t, n - 1)
                for b in range(half * NB // 2, (half + 1) * NB // 2):
                    cf = coef[l][:, bass.ds(c, 1), b:b + 1].rearrange("p a b -> p (a b)")
                    if b == 0:
                        i = nc.vector.tensor_scalar(msg[:, s, :], ps_b[s][:, b, :], cf, None, ALU.mult)
                    else:
                        dve.wait_ge(linked, links + b)
                        i = nc.vector.scalar_tensor_tensor(out=msg[:, s, :], in0=ps_b[s][:, b, :], scalar=cf,
                                                           in1=msg[:, s, :], op0=ALU.mult, op1=ALU.add)
                    if b == NB // 2 - 1:
                        i.then_inc(halved, 1)
                        dve.wait_ge(halved, n + 1)
                    elif b < NB - 1:
                        i.then_inc(linked, 1)
                    else:
                        i.then_inc(msg_made, 1)

            def scan(c, s, n, first):
                wait(dve, msg_t, n + 1)
                wait(dve, run_t, n - 1)
                if not first:
                    wait(dve, scanned, n)
                nc.vector.tensor_tensor_scan(run[:, s, :], same[:, bass.ds(c * P, P)], ps_m[:, 0, :],
                                             0.0 if first else run[:, 1 - s, P - 1:P],
                                             ALU.mult, ALU.add).then_inc(scanned, 1)

            def move_y(l, h, b, j, nj=Q, tail=0):
                wait(dve, y_made, h + 1)
                def move(rows, j, nj, q):
                    o = yout[0:rows, b, j:j + nj, :]
                    y = ps_y[0:rows, q * D:(q + nj) * D].rearrange("p (j d) -> p j d", d=D)
                    if l == 0:
                        return nc.vector.tensor_copy(o, y)
                    return nc.vector.tensor_tensor(o, y, bias2_b[0:rows, :].unsqueeze(1).to_broadcast([rows, nj, D]), ALU.add)
                i = move(P, j, nj, 0)
                if tail:
                    i = move(tail, j + nj, 1, nj)
                i.then_inc(y_moved, 1)

            for l in range(2):
                L = l * CH
                H = l * HALVES

                def step_m(it, u, m_, c_, dense, l=l, L=L, H=H):
                    n = it * U + (L + u - 1)
                    links = it * (U * 6) + (L + u - 1) * 6
                    if m_:
                        messages(it * U + (u - 1), (u + 1) % 2, l, n, links, 0)
                    if dense == 2 or (dense and not (isinstance(it, int) and it == 0 and u == 0)):
                        pb = (u + 1) % 2
                        move_y(l, it * (2 * U) + (H + 2 * u - 1), pb, Q)
                    if m_:
                        messages(it * U + (u - 1), (u + 1) % 2, l, n, links - 1, 1)
                    if c_:
                        scan(it * U + (u - 2), u % 2, it * U + (L + u - 2), isinstance(it, int) and it * U + u - 2 == 0)
                    if dense == 1:
                        b = u % 2
                        wait(dve, y_out[b], it * (16 * U // 2) + (16 * (u // 2) + (y_total(b, 0) if l else 0)))
                        move_y(l, it * (2 * U) + (H + 2 * u), b, 0)

                for u in range(U):
                    step_m(0, u, u >= 1, u >= 2, 1)
                with dve.Fori(1, DTURNS) as it:
                    for u in range(U):
                        step_m(it, u, True, True, 1)
                move_y(l, H + 2 * NBLK - 1, 1, Q)
                dve.wait_ge(y_out[0], y_total(0, l) - 32)
                move_y(l, H + 2 * NBLK, 0, 0)
                move_y(l, H + 2 * NBLK + 1, 0, Q, TAILQ - Q, TAIL)
                with dve.Fori(DTURNS, TURNS) as it:
                    for u in range(U):
                        step_m(it, u, True, True, 0)
                step_m(TURNS, 0, True, True, 0)
                step_m(TURNS, 1, False, True, 0)
                if l == 0:
                    step(nc.vector.memset(coef[1][:, :, :], 0.0))
                    for b in range(NBUF):
                        dve.wait_ge(y_out[b], y_total(b, 0))
                    coefficients(1)
                    dve.wait_ge(coef_ok, 2)

            fstat = stage_stats(dve)
            last_vector(dve, fstat)

        @block.scalar
        def _(act):
            act.wait_ge(weights_in, 16 * 8)

            def stage_rows(c, u, n, turn16):
                wait(act, gathered[u % U], turn16)
                wait(act, gt_made, n - 1)
                nc.scalar.copy(stage[:, u % 2, :],
                               sums[:, bass.ds(c, 1), :].rearrange("p a d -> p (a d)")).then_inc(staged, 1)

            def move_t(l, o, i):
                if l == 0:
                    return nc.scalar.copy(o, i)
                return nc.scalar.activation(o, i, ACT.Relu, bias=bias1_c[:, 0:1])

            def move_run(c, n):
                wait(act, run_t, n + 1)
                nc.scalar.copy(sums[:, bass.ds(c, 1), :].rearrange("p a d -> p (a d)"), ps_g[:, 1, :]).then_inc(summed, 1)

            def move_x(l, h, s, cols=Q * P):
                wait(act, xt_made, h + 1)
                wait(act, y_made, h - 1)
                move_t(l, xT[:, s, 0:cols], ps_x[:, 0:cols]).then_inc(xt_moved, 1)

            for l in range(2):
                L = l * CH
                H = l * HALVES

                def step_m(it, u, next_, a_, d_, dense, l=l, L=L, H=H):
                    if next_:
                        v = (u + 1) % U
                        it_ = it if u + 1 < U else it + 1
                        stage_rows(it * U + (u + 1), v, it * U + (L + u + 1), it_ * 16 + (16 + 16 * l * TURNS))
                    if d_:
                        if a_:
                            wait(act, gt_made, it * U + (L + u + 1))
                        move_run(it * U + (u - 4), it * U + (L + u - 4))
                    if a_:
                        n = it * U + (L + u)
                        wait(act, gt_made, n + 1)
                        wait(act, based, n * 2 - 2)
                        move_t(l, gT[:, u % 2, :], ps_g[:, 0, :]).then_inc(gt_moved, 1)
                    if dense:
                        for q in range(2):
                            move_x(l, it * (2 * U) + (H + 2 * u + q), q)

                stage_rows(0, 0, L, 16 + 16 * l * TURNS)
                for u in range(U):
                    step_m(0, u, True, True, False, True)
                with act.Fori(1, DTURNS) as it:
                    for u in range(U):
                        step_m(it, u, True, True, True, True)
                move_x(l, H + 2 * NBLK, 0)
                move_x(l, H + 2 * NBLK + 1, 1, (TAILQ - Q) * P + TAIL)
                with act.Fori(DTURNS, TURNS - 1) as it:
                    for u in range(U):
                        step_m(it, u, True, True, True, False)
                for u in range(U):
                    step_m(TURNS - 1, u, u < U - 1, True, True, False)
                for u in range(4):
                    step_m(TURNS, u, False, False, True, False)

            f = stage_stats(None)

            def one(k, b, rows=P, nj=FJ):
                h, xx = final_tiles(b)
                act.wait_ge(f_var, k * 4 + 3)
                nc.scalar.activation(f["q"][b][0:rows, 0:nj], f["v"][b][0:rows, 0:nj], ACT.Sqrt).then_inc(f_std, 1)
                act.wait_ge(f_norm, k + 1)
                for j in range(nj):
                    i = nc.scalar.activation(xx[0:rows, j, :], h[0:rows, j, :], ACT.Identity,
                                             bias=f["o"][b][0:rows, j:j + 1], scale=f["r"][b][0:rows, j:j + 1])
                i.then_inc(f_done, 1)

            with act.Fori(0, FN // FBUF) as r:
                for b in range(FBUF):
                    one(r * FBUF + b, b)
            one(FN, 0, TAIL, 1)

        @block.tensor
        def _(pe):
            pe.wait_ge(ident_ok, 2)
            pe.wait_ge(vdone, 12)
            pe.wait_ge(vdone, 12)
            homes = {"src": (0, 0), "dst": (0, 4), "last": (1, 0), "rel": (1, 4)}
            for k, (s, a) in homes.items():
                o = ps_b[s][:, a:a + 4, :].rearrange("p a d -> p (a d)")
                nc.tensor.transpose(o[:, 0:P], val[k][:, 0, :], ident[:, :])
                nc.tensor.transpose(o[:, P:CH], val[k][0:CH - P, 1, :], ident[0:CH - P, 0:CH - P])
            nc.tensor.matmul(ps_m[0:1, 0, 0:1], ones_c, worst, start=True, stop=True).then_inc(setup_t, 1)
            pe.wait_ge(weights_in, 16 * 8)
            pe.wait_ge(idx_ok, 1)

            for l in range(2):
                L = l * CH
                H = l * HALVES
                bl = basis[l][:, :, :].rearrange("p b d -> p (b d)")

                def node_t(h, s, b, j, tiles=Q, tail=0, x_count=None, l=l):
                    if x_count is not None:
                        pe.wait_ge(x_in[b], x_count)
                    wait(pe, xt_moved, h)
                    for q in range(tiles):
                        i = nc.tensor.transpose(ps_x[:, q * P:(q + 1) * P], xin[:, b, j + q, :], ident[:, :])
                    if tail:
                        i = nc.tensor.transpose(ps_x[:, tiles * P:tiles * P + tail], xin[0:tail, b, j + tiles, :],
                                                ident[0:tail, 0:tail])
                    i.then_inc(xt_made, 1)

                def node_mm(h, s, tiles=Q, tail=0, l=l):
                    wait(pe, xt_moved, h + 1)
                    wait(pe, y_moved, h)
                    for q in range(tiles):
                        i = nc.tensor.matmul(ps_y[:, q * D:(q + 1) * D], xT[:, s, q * P:(q + 1) * P],
                                             loop_w[l][:, :], start=True, stop=True)
                    if tail:
                        i = nc.tensor.matmul(ps_y[0:tail, tiles * D:(tiles + 1) * D],
                                             xT[:, s, tiles * P:tiles * P + tail],
                                             loop_w[l][:, :], start=True, stop=True)
                    i.then_inc(y_made, 1)

                def times_bases(n, s, half, bl=bl):
                    o = ps_b[s][:, :, :].rearrange("p b d -> p (b d)")
                    w = NB // 2 * D
                    if half == 0:
                        wait(pe, msg_made, n - 1)
                    nc.tensor.matmul(o[:, half * w:(half + 1) * w], gT[:, s, :], bl[:, half * w:(half + 1) * w],
                                     start=True, stop=True).then_inc(based, 1)

                def step_m(it, u, a_, b_, c_, d_, dense, l=l, L=L, H=H):
                    m = it * U + (L + u)
                    wait(pe, gt_moved, m if a_ or b_ else L + CH)
                    wait(pe, summed, m - 4 if d_ else (L if l else 0))
                    if d_:
                        wait(pe, scanned, m - 3)
                    if a_:
                        wait(pe, staged, m + 1)
                        if d_:
                            nc.tensor.transpose(ps_g[:, 1, :], run[:, u % 2, :], ident[:, :]).then_inc(run_t, 1)
                        nc.tensor.transpose(ps_g[:, 0, :], stage[:, u % 2, :], ident[:, :]).then_inc(gt_made, 1)
                    elif d_:
                        nc.tensor.transpose(ps_g[:, 1, :], run[:, u % 2, :], ident[:, :]).then_inc(run_t, 1)
                    if b_:
                        times_bases(m - 1, (u + 1) % 2, 0)
                    if c_:
                        wait(pe, msg_made, m - 1)
                        wait(pe, scanned, m - 2)
                        nc.tensor.transpose(ps_m[:, 0, :], msg[:, u % 2, :], ident[:, :]).then_inc(msg_t, 1)
                    h = it * (2 * U) + (H + 2 * u)
                    if dense:
                        node_t(h, 0, u % 2, 0, x_count=it * (16 * U // 2)
                               + (16 * (u // 2 + 1) + (y_total(u % 2, 0) if l else 0)))
                        if not (isinstance(it, int) and it == 0 and u == 0):
                            node_mm(h - 1, 1)
                    if b_:
                        times_bases(m - 1, (u + 1) % 2, 1)
                    if dense:
                        node_t(h + 1, 1, u % 2, Q)
                        node_mm(h, 0)

                for u in range(U):
                    step_m(0, u, True, u >= 1, u >= 2, False, True)
                with pe.Fori(1, DTURNS) as it:
                    for u in range(U):
                        step_m(it, u, True, True, True, True, True)
                h = H + 2 * NBLK
                node_t(h, 0, 0, 0, x_count=y_total(0, l))
                node_mm(h - 1, 1)
                node_t(h + 1, 1, 0, Q, TAILQ - Q, TAIL)
                node_mm(h, 0)
                node_mm(h + 1, 1, TAILQ - Q, TAIL)
                with pe.Fori(DTURNS, TURNS) as it:
                    for u in range(U):
                        step_m(it, u, True, True, True, True, False)
                step_m(TURNS, 0, False, True, True, True, False)
                step_m(TURNS, 1, False, False, True, True, False)
                step_m(TURNS, 2, False, False, False, True, False)
                step_m(TURNS, 3, False, False, False, True, False)


_INS = ['x', 'src', 'dst', 'edge_type_16', 'L0_gnn_basis1', 'L0_gnn_w_comp1', 'L0_gnn_loop_w1', 'L0_gnn_bias1',
        'L0_gnn_basis2', 'L0_gnn_w_comp2', 'L0_gnn_loop_w2', 'L0_gnn_bias2']


def kernel(**inputs):
    import numpy as _np
    import concourse.bacc as _bacc
    from concourse import mybir as _mybir
    from concourse.bass_utils import run_bass_kernel_spmd as _run

    nc = _bacc.Bacc("TRN2", target_bir_lowering=False, num_devices=1)
    arrays, args = {}, []
    for name in _INS:
        a = _np.ascontiguousarray(inputs[name])
        arrays[f"in_{name}"] = a
        args.append(nc.dram_tensor(f"in_{name}", a.shape, _mybir.dt.from_np(a.dtype), kind="ExternalInput").ap())
    args.append(nc.dram_tensor("out_rows", (N, D), _mybir.dt.float32, kind="ExternalOutput").ap())
    build_rgcn(nc, *args)
    r = _run(nc, [arrays], core_ids=[0])
    return r.results[0]["out_rows"]
```

```python
from contextlib import ExitStack

import concourse.bass as bass
from concourse import mybir

F32 = mybir.dt.float32
BF16 = mybir.dt.bfloat16
I32 = mybir.dt.int32
ALU = mybir.AluOpType
ACT = mybir.ActivationFunctionType
AX = mybir.AxisListType

P = 128
N = 50000
E = 25000
D = 128
NREL = 16
NB = 8

CH = -(-E // P)
U = 4
G = 2
PAIRS = CH // 2
TURNS = PAIRS // G
LAG = 4
FULL = E // P
REST = E - FULL * P
HALF1 = FULL - P

J = 8
Q = 4
BLK = J * P
NBLK = N // BLK
TAILQ = (N - NBLK * BLK) // P
TAIL = N - NBLK * BLK - TAILQ * P
NBUF = 2
DTURNS = NBLK // G
HALVES = 2 * NBLK + 2

SC = 14
DUMMY = N
SLOW = DUMMY + SC * P
ROWS = SLOW + P

FJ = 13
FBLK = FJ * P
FN = N // FBLK
FBUF = 6
LEAD = 4
EPS = 1e-5


def build_rgcn(nc, x, src, dst, rel, basis1, w_comp1, loop_w1, bias1,
               basis2, w_comp2, loop_w2, bias2, out):
    ctx = ExitStack()
    with ctx:
        def sb(name, shape, dt=F32):
            return ctx.enter_context(nc.sbuf_tensor(name, shape, dt))

        def ps(name, shape):
            return ctx.enter_context(nc.psum_tensor(name, shape, F32))

        def sem(name):
            return ctx.enter_context(nc.semaphore(name))

        nodes = [nc.dram_tensor(f"nodes{l}", (ROWS, D), F32).ap() for l in range(2)]
        same_d = nc.dram_tensor("same_d", (CH * P,), BF16).ap()

        sums = sb("sums", [P, CH, D])
        same = sb("same", [P, CH * P], BF16)
        coef = [sb(f"coef{l}", [P, CH, NB]) for l in range(2)]
        src_i = sb("src_i", [P, CH], I32)
        coef_now = sb("coef_now", [P, 2, 2 * NB])
        put_i = sb("put_i", [P, CH], I32)
        dst_f = sb("dst_f", [P, CH])
        last_f = sb("last_f", [P, CH])
        rel_f = sb("rel_f", [P, CH])
        basis = [sb(f"basis{l}", [P, NB, D]) for l in range(2)]
        loop_w = [sb(f"loop_w{l}", [P, D]) for l in range(2)]
        ident = sb("ident", [P, P])
        bias1_c = sb("bias1_c", [P, 1])
        bias2_b = sb("bias2_b", [P, D])
        w_b = [sb(f"w_b{l}", [P, NREL * NB]) for l in range(2)]
        rel_no = sb("rel_no", [P, NREL])
        unsorted_i = sb("unsorted_i", [1, 1], I32)
        xin = sb("xin", [P, NBUF, J, D])
        yout = sb("yout", [P, NBUF, J, D])
        stage = sb("stage", [P, 2, D])
        gT = sb("gT", [P, 2, 2, P])
        msg = sb("msg", [P, 2, 2, D])
        run = sb("run", [P, 2, 2 * P])
        eq_f = sb("eq_f", [P, CH])
        xT = sb("xT", [P, 2, Q * P])

        def scratch(first, chunks):
            return sums[:, first:first + chunks, :]
        raw = {k: scratch(CH - 20 + 2 * i, 2).bitcast(I32) for i, k in enumerate(("src", "dst", "nxt", "prv", "rel"))}
        val = {k: scratch(CH - 10 + 2 * i, 2) for i, k in enumerate(("src", "dst", "last", "rel"))}
        bigger = scratch(CH - 2, 2)
        dummy_i = sums[:, CH - 22:CH - 20, :].rearrange("p a d -> p (a d)")[:, 0:CH].bitcast(I32)
        away = sums[:, CH - 24:CH - 22, :].rearrange("p a d -> p (a d)")[:, 0:CH]
        same_h = sums[:, CH - 25, :].bitcast(BF16).rearrange("p (a d) -> p a d", a=2)
        zeros = scratch(CH - 40, SC + 1)
        rel_no_i = sums[:, CH - 46, 32:32 + NREL].bitcast(I32)
        ones_c = sums[:, CH - 46, 64:65]
        worst = sums[:, CH - 46, 65:66]

        col_b = xin[:, 0, 0, :]
        joins = xin[:, 0, 1, :]
        after = xin[:, 0, 2, :]
        later_m = xin[:, 0, 3, :]
        slow_row = xin[:, 0, 4, 0:1]
        later = xin[:, 0, 4, 1:2]
        away_s = xin[:, 0, 4, 2:3]
        slow_row_i = xin[:, 0, 4, 3:4].bitcast(I32)
        slow_put_i = yout[:, 0, 0, 0:1].bitcast(I32)
        whole = yout[:, 0, 1, :]

        ps_g = ps("ps_g", [P, 4, P])
        ps_m = ps("ps_m", [P, 4, P])
        ps_x = ps("ps_x", [P, Q * P])
        ps_y = ps("ps_y", [P, Q * D])
        ps_b = [ps(f"ps_b{h}", [P, 2, NB // 2, D]) for h in range(2)]

        cleared = sem("cleared")
        idx_in = sem("idx_in")
        weights_in = sem("weights_in")
        ident_ok = sem("ident_ok")
        iota_ok = sem("iota_ok")
        vdone = sem("vdone")
        setup_t = sem("setup_t")
        idx_ok = sem("idx_ok")
        eq_ok = sem("eq_ok")
        coef_ok = sem("coef_ok")
        same_w = sem("same_w")
        same_in = sem("same_in")
        zero_w = sem("zero_w")
        gathered = [sem(f"gathered{u}") for u in range(U)]
        staged = sem("staged")
        coef_set = sem("coef_set")
        gt_made = sem("gt_made")
        gt_moved = sem("gt_moved")
        based = sem("based")
        linked = sem("linked")
        msg_t = sem("msg_t")
        scanned = sem("scanned")
        run_t = sem("run_t")
        summed = sem("summed")
        x_in = [sem(f"x_in{b}") for b in range(NBUF)]
        xt_made = sem("xt_made")
        xt_moved = sem("xt_moved")
        y_made = sem("y_made")
        y_moved = sem("y_moved")
        y_out = [sem(f"y_out{b}") for b in range(NBUF)]
        put = [sem(f"put{u}") for u in range(SC)]
        slow_mask = sem("slow_mask")
        slow_col = sem("slow_col")
        slow_dst = sem("slow_dst")
        slow_join = sem("slow_join")
        slow_sum = sem("slow_sum")
        slow_v = sem("slow_v")
        slow_ready = sem("slow_ready")
        slow_put = sem("slow_put")
        layer_put = sem("layer_put")
        f_in = [sem(f"f_in{b}") for b in range(FBUF)]
        f_bias = sem("f_bias")
        f_sum = sem("f_sum")
        f_stat = sem("f_stat")
        f_var = sem("f_var")
        f_std = sem("f_std")
        f_norm = sem("f_norm")
        f_done = sem("f_done")
        f_out = [sem(f"f_out{b}") for b in range(FBUF)]


        def y_total(b, l):
            return 16 * (NBLK // NBUF + 2 * (b == 0)) * (l + 1)

        def put_total(u, l):
            return 16 * (l + 1) * (CH // SC)

        def node_block(k, l):
            t = x if l == 0 else nodes[0]
            return t[bass.ds(k * BLK, BLK), :].rearrange("(p j) d -> p j d", j=J)

        def wait(eng, s, v):
            if not isinstance(v, int) or v > 0:
                eng.wait_ge(s, v)

        def final_tiles(b):
            h = sums[:, 2 * FJ * b:2 * FJ * b + FJ, :]
            xx = sums[:, 2 * FJ * b + FJ:2 * FJ * (b + 1), :]
            return h, xx

        def last_load(sp):
            def load(k, b):
                h, xx = final_tiles(b)
                sp.dma_start(h, nodes[1][bass.ds(k * FBLK, FBLK), :].rearrange("(p j) d -> p j d", j=FJ)).then_inc(f_in[b], 16)
                sp.dma_start(xx, x[bass.ds(k * FBLK, FBLK), :].rearrange("(p j) d -> p j d", j=FJ)).then_inc(f_in[b], 16)

            def store(k, b):
                h, xx = final_tiles(b)
                sp.wait_ge(f_done, k + 1)
                sp.dma_start(out[bass.ds(k * FBLK, FBLK), :].rearrange("(p j) d -> p j d", j=FJ), xx).then_inc(f_out[b], 16)

            for b in range(LEAD):
                load(b, b)
            for b in range(FBUF - LEAD):
                store(b, b)
                load(b + LEAD, b + LEAD)
            with sp.Fori(0, FN // FBUF - 1) as r:
                for b in range(FBUF):
                    k = r * FBUF + (b + FBUF - LEAD)
                    store(k, (b + FBUF - LEAD) % FBUF)
                    sp.wait_ge(f_out[b], r * 16 + 16)
                    load(k + LEAD, b)
            for k in range(FN - LEAD, FN):
                store(k, k % FBUF)
            h, xx = final_tiles(0)
            sp.wait_ge(f_out[0], 16 * (FN // FBUF))
            sp.dma_start(h[0:TAIL, 0, :], nodes[1][N - TAIL:N, :]).then_inc(f_in[0], 16)
            sp.dma_start(xx[0:TAIL, 0, :], x[N - TAIL:N, :]).then_inc(f_in[0], 16)
            sp.wait_ge(f_done, FN + 1)
            sp.dma_start(out[N - TAIL:N, :], xx[0:TAIL, 0, :]).then_inc(f_out[0], 16)
            for b in range(FBUF):
                sp.wait_ge(f_out[b], 16 * (FN // FBUF + (b == 0)))

        def stage_stats(dve):
            return {
                "bn": [sums[:, 2 * FJ * FBUF + b, 0:6 * FJ].rearrange("p (j s) -> p j s", s=6) for b in range(FBUF)],
                "s": [sums[:, 2 * FJ * FBUF + FBUF + b, 0:FJ] for b in range(FBUF)],
                "d": [sums[:, 2 * FJ * FBUF + FBUF + b, 16:16 + FJ] for b in range(FBUF)],
                "q": [sums[:, 2 * FJ * FBUF + FBUF + b, 32:32 + FJ] for b in range(FBUF)],
                "v": [sums[:, 2 * FJ * FBUF + FBUF + b, 48:48 + FJ] for b in range(FBUF)],
                "r": [sums[:, 2 * FJ * FBUF + FBUF + b, 64:64 + FJ] for b in range(FBUF)],
                "o": [sums[:, 2 * FJ * FBUF + FBUF + b, 80:80 + FJ] for b in range(FBUF)],
            }

        def last_vector(dve, f):
            def add_rows(k, b, rows, nj, turn):
                h, xx = final_tiles(b)
                dve.wait_ge(f_in[b], turn * 32 + 32)
                dve.wait_ge(f_bias, k + 1)
                hv, xv = (a[0:rows, 0:nj, :].rearrange("p j d -> p (j d)") for a in (h, xx))
                nc.vector.scalar_tensor_tensor(out=hv, in0=hv, scalar=0.0, in1=xv,
                                               op0=ALU.max, op1=ALU.add).then_inc(f_sum, 1)

            def stats(k, b, rows, nj, j0, j1, first):
                h, xx = final_tiles(b)
                if first:
                    dve.wait_ge(f_sum, k + 1)
                for j in range(j0, j1):
                    i = nc.vector.bn_stats(f["bn"][b][0:rows, j, :], h[0:rows, j, :])
                i.then_inc(f_stat, 2 if nj == 1 else 1)

            def small(k, b, rows, nj):
                g = {n: f[n][b][0:rows, 0:nj] for n in "sdqvro"}
                bn = f["bn"][b][0:rows, 0:nj, :]
                dve.wait_ge(f_stat, k * 2 + 2)
                nc.vector.tensor_tensor(g["d"], bn[:, :, 1], bn[:, :, 4], ALU.subtract)
                nc.vector.tensor_tensor(g["q"], bn[:, :, 2], bn[:, :, 5], ALU.add)
                nc.vector.tensor_tensor(g["s"], bn[:, :, 1], bn[:, :, 4], ALU.add).then_inc(f_var, 1)
                dve.wait_ge(f_var, k * 4 + 1)
                nc.vector.tensor_tensor(g["d"], g["d"], g["d"], ALU.mult)
                nc.vector.tensor_scalar(g["q"], g["q"], 1.0 / D, EPS, ALU.mult, ALU.add).then_inc(f_var, 1)
                dve.wait_ge(f_var, k * 4 + 2)
                nc.vector.scalar_tensor_tensor(out=g["v"], in0=g["d"], scalar=0.25, in1=g["q"],
                                               op0=ALU.mult, op1=ALU.add).then_inc(f_var, 1)

            def scale(k, b, rows, nj, part):
                g = {n: f[n][b][0:rows, 0:nj] for n in "sdqvro"}
                if part == 0:
                    dve.wait_ge(f_std, k + 1)
                    nc.vector.reciprocal(g["r"], g["q"]).then_inc(f_var, 1)
                else:
                    dve.wait_ge(f_var, k * 4 + 4)
                    nc.vector.scalar_tensor_tensor(out=g["o"], in0=g["s"], scalar=-0.5, in1=g["r"],
                                                   op0=ALU.mult, op1=ALU.mult).then_inc(f_norm, 1)

            def block_k(k, b, turn, rows=P, nj=FJ, before=True, rows_b=P, nj_b=FJ):
                add_rows(k, b, rows, nj, turn)
                if before:
                    scale(k - 1, (b + FBUF - 1) % FBUF, rows_b, nj_b, 0)
                half = (nj + 1) // 2
                stats(k, b, rows, nj, 0, half, True)
                if before:
                    scale(k - 1, (b + FBUF - 1) % FBUF, rows_b, nj_b, 1)
                if nj > 1:
                    stats(k, b, rows, nj, half, nj, False)
                small(k, b, rows, nj)

            for b in range(FBUF):
                block_k(b, b, 0, before=b > 0)
            with dve.Fori(1, FN // FBUF) as r:
                for b in range(FBUF):
                    block_k(r * FBUF + b, b, r)
            for part in range(2):
                scale(FN - 1, (FN - 1) % FBUF, P, FJ, part)
            block_k(FN, 0, FN // FBUF, TAIL, 1, before=False)
            scale(FN, 0, TAIL, 1, 0)
            scale(FN, 0, TAIL, 1, 1)

        block = ctx.enter_context(nc.Block())

        @block.sync
        def _(sp):
            def load_edges(tile, a, shift):
                cut = P * P + shift
                if shift < 0:
                    sp.dma_start(tile[0:1, 0, 1:P], a[0:P - 1].rearrange("(p j) -> p j", p=1)).then_inc(idx_in, 16)
                    sp.dma_start(tile[1:P, 0, :], a[P - 1:cut].rearrange("(p j) -> p j", j=P)).then_inc(idx_in, 16)
                else:
                    sp.dma_start(tile[:, 0, :], a[shift:cut].rearrange("(p j) -> p j", j=P)).then_inc(idx_in, 16)
                end = cut + HALF1 * P
                left = min(REST, E - end)
                sp.dma_start(tile[0:HALF1, 1, :], a[cut:end].rearrange("(p j) -> p j", j=P)).then_inc(idx_in, 16)
                sp.dma_start(tile[HALF1:HALF1 + 1, 1, 0:left],
                             a[end:end + left].rearrange("(p j) -> p j", p=1)).then_inc(idx_in, 16)

            sp.wait_ge(cleared, 1)
            load_edges(raw["src"], src, 0)
            load_edges(raw["dst"], dst, 0)
            load_edges(raw["nxt"], dst, 1)
            load_edges(raw["prv"], dst, -1)
            load_edges(raw["rel"], rel, 0)

            sp.dma_start(w_b[0][:, :], w_comp1.rearrange("r b -> (r b)").partition_broadcast(P)).then_inc(weights_in, 16)
            sp.dma_start(w_b[1][:, :], w_comp2.rearrange("r b -> (r b)").partition_broadcast(P)).then_inc(weights_in, 16)
            sp.dma_start(basis[0][:, :, :], basis1.rearrange("b i o -> i b o")).then_inc(weights_in, 16)
            sp.dma_start(basis[1][:, :, :], basis2.rearrange("b i o -> i b o")).then_inc(weights_in, 16)
            sp.dma_start(loop_w[0][:, :], loop_w1).then_inc(weights_in, 16)
            sp.dma_start(loop_w[1][:, :], loop_w2).then_inc(weights_in, 16)
            sp.dma_start(bias1_c[:, :], bias1.rearrange("(p a) -> p a", a=1)).then_inc(weights_in, 16)
            sp.dma_start(bias2_b[:, :], bias2.partition_broadcast(P)).then_inc(weights_in, 16)
            for l in range(2):
                sp.dma_start(nodes[l][DUMMY:ROWS, :].rearrange("(s p) d -> p s d", p=P), zeros[:, :, :]).then_inc(zero_w, 16)
            sp.wait_ge(same_w, 1)
            sp.dma_start(same_d[0:P * P].rearrange("(p j) -> p j", j=P), same_h[:, 0, :]).then_inc(same_w, 16)
            sp.dma_start(same_d[P * P:CH * P].rearrange("(p j) -> p j", j=P), same_h[0:CH - P, 1, :]).then_inc(same_w, 16)
            sp.wait_ge(same_w, 33)
            sp.dma_start(same[:, :], same_d.partition_broadcast(P)).then_inc(same_in, 16)

            for l in range(2):
                if l == 1:
                    sp.wait_ge(layer_put, 1)
                for b in range(NBUF):
                    sp.dma_start(xin[:, b, :, :], node_block(b, l)).then_inc(x_in[b], 16)
                h0 = l * HALVES

                def move_block(k, b, more):
                    if more:
                        sp.wait_ge(xt_made, k * 2 + (h0 + 2))
                        sp.dma_start(xin[:, b, :, :], node_block(k + NBUF, l)).then_inc(x_in[b], 16)
                    sp.wait_ge(y_moved, k * 2 + (h0 + 2))
                    sp.dma_start(nodes[l][bass.ds(k * BLK, BLK), :].rearrange("(p j) d -> p j d", j=J),
                                 yout[:, b, :, :]).then_inc(y_out[b], 16)

                with sp.Fori(0, NBLK // NBUF - 1) as r:
                    for b in range(NBUF):
                        move_block(r * NBUF + b, b, True)
                t = x if l == 0 else nodes[0]
                lo = NBLK * BLK
                mid = lo + TAILQ * P
                sp.wait_ge(xt_made, h0 + 2 * (NBLK - 1))
                sp.dma_start(xin[:, 0, 0:TAILQ, :], t[lo:mid, :].rearrange("(p j) d -> p j d", j=TAILQ)).then_inc(x_in[0], 16)
                sp.dma_start(xin[0:TAIL, 0, TAILQ, :], t[mid:N, :]).then_inc(x_in[0], 16)
                for b in range(NBUF):
                    move_block(NBLK - NBUF + b, b, False)
                sp.wait_ge(y_moved, h0 + HALVES)
                sp.dma_start(nodes[l][lo:mid, :].rearrange("(p j) d -> p j d", j=TAILQ),
                             yout[:, 0, 0:TAILQ, :]).then_inc(y_out[0], 16)
                sp.dma_start(nodes[l][mid:N, :], yout[0:TAIL, 0, TAILQ, :]).then_inc(y_out[0], 16)

            sp.wait_ge(layer_put, 2)
            last_load(sp)

        @block.gpsimd
        def _(pool):
            limit = pool.snap(pool.to_reg(ROWS - 1))
            pool.memset(ident[:, :], 0.0).then_inc(ident_ok, 1)
            pool.wait_ge(ident_ok, 1)
            pool.affine_select(out=ident[:, :], in_=ident[:, :], compare_op=ALU.not_equal, fill=1.0,
                               base=0, pattern=[[-1, P]], channel_multiplier=1).then_inc(ident_ok, 1)
            pool.iota(dummy_i, pattern=[[0, CH // SC], [P, SC]], base=DUMMY, channel_multiplier=1).then_inc(iota_ok, 1)
            pool.iota(rel_no_i, pattern=[[1, NREL]], base=0, channel_multiplier=0).then_inc(iota_ok, 1)
            pool.wait_ge(idx_ok, 1)
            unsorted = pool.value_load(unsorted_i[0:1, 0:1], min_val=0, max_val=E)

            def slow_scatters(l):
                pool.iota(slow_row_i, pattern=[[0, 1]], base=SLOW, channel_multiplier=1).then_inc(slow_mask, 1)
                pool.memset(later_m, 1.0).then_inc(slow_mask, 1)
                pool.wait_ge(slow_mask, 3 * l + 2)
                pool.affine_select(out=later_m, in_=later_m, compare_op=ALU.is_gt, fill=0.0, base=0,
                                   pattern=[[1, P]], channel_multiplier=-1).then_inc(slow_mask, 1)
                with pool.Fori(l * CH + 1, l * CH + CH + 1) as n:
                    pool.wait_ge(slow_ready, n)
                    pool.nop(nofuse=True)
                    pool.indirect_dma_start(
                        out=nodes[l][:, :], out_offset=bass.IndirectOffsetOnAxis(ap=slow_put_i, axis=0),
                        in_=whole, in_offset=None, bounds_check=limit, oob_is_err=True,
                        compute_op=ALU.add).then_inc(slow_put, 16)
                    done = pool.snap(n * 16)
                    pool.wait_ge(slow_put, done)
                    pool.nop(nofuse=True)

            def scatter(l, c):
                if c % 2 == 0:
                    pool.wait_ge(summed, l * PAIRS + c // 2 + 1)
                if l * CH + c >= SC:
                    pool.wait_ge(put[c % SC], 16 * (l * (CH // SC) + c // SC))
                pool.indirect_dma_start(
                    out=nodes[l][:, :], out_offset=bass.IndirectOffsetOnAxis(ap=put_i[:, c:c + 1], axis=0),
                    in_=sums[:, c, :], in_offset=None, bounds_check=limit, oob_is_err=True,
                    compute_op=ALU.add).then_inc(put[c % SC], 16)

            for l in range(2):
                table = x if l == 0 else nodes[0]
                for c in range(CH):
                    if l == 0 and c == CH - 46:
                        pool.wait_ge(idx_ok, 1)
                        pool.wait_ge(zero_w, 32)
                        pool.wait_ge(same_w, 33)
                        pool.wait_ge(setup_t, 1)
                    if l * CH + c >= U:
                        turn = l * TURNS + c // U
                        pool.wait_ge(gathered[c % U], 16 * turn)
                    pool.indirect_dma_start(
                        out=sums[:, c, :], out_offset=None, in_=table[:, :],
                        in_offset=bass.IndirectOffsetOnAxis(ap=src_i[:, c:c + 1], axis=0)).then_inc(gathered[c % U], 16)
                for b in range(NBUF):
                    pool.wait_ge(y_out[b], y_total(b, l))
                with pool.If(unsorted < 1):
                    for c in range(CH):
                        scatter(l, c)
                    for u in range(SC):
                        pool.wait_ge(put[u], put_total(u, l))
                with pool.If(unsorted > 0):
                    slow_scatters(l)
                pool.sem_inc(layer_put, 1)

            def add_bias(k, b, turn, rows=P, nj=FJ):
                h, xx = final_tiles(b)
                pool.wait_ge(f_in[b], turn * 32 + 32)
                nc.gpsimd.tensor_tensor(h[0:rows, 0:nj, :], h[0:rows, 0:nj, :],
                                        bias2_b[0:rows, :].unsqueeze(1).to_broadcast([rows, nj, D]),
                                        ALU.add).then_inc(f_bias, 1)

            with pool.Fori(0, FN // FBUF) as r:
                for b in range(FBUF):
                    add_bias(r * FBUF + b, b, r)
            add_bias(FN, 0, FN // FBUF, TAIL, 1)

        @block.vector
        def _(dve):
            steps = [0]

            def step(ins):
                steps[0] += 1
                ins.then_inc(vdone, 1)
                dve.wait_ge(vdone, steps[0])

            step(nc.vector.memset(raw["src"], 0))
            step(nc.vector.memset(raw["dst"], DUMMY))
            step(nc.vector.memset(raw["nxt"], DUMMY))
            step(nc.vector.memset(raw["prv"], -1))
            step(nc.vector.memset(zeros, 0.0))
            step(nc.vector.memset(ones_c, 1.0))
            nc.vector.memset(raw["rel"], 0).then_inc(cleared, 1)
            dve.wait_ge(idx_in, 16 * 16)
            step(nc.vector.tensor_copy(val["src"], raw["src"]))
            step(nc.vector.tensor_copy(val["dst"], raw["dst"]))
            step(nc.vector.tensor_copy(val["rel"], raw["rel"]))
            step(nc.vector.tensor_tensor(val["last"], raw["dst"], raw["nxt"], ALU.not_equal))
            nc.vector.tensor_tensor(same_h, raw["dst"], raw["prv"], ALU.is_equal).then_inc(same_w, 1)
            step(nc.vector.tensor_tensor(bigger, raw["dst"], raw["nxt"], ALU.is_gt))
            step(nc.vector.reduce_sum(worst, bigger.rearrange("p a d -> p (a d)"), axis=AX.X))
            dve.wait_ge(setup_t, 1)
            step(nc.vector.tensor_copy(src_i[:, :], ps_b[0][:, 0, :, :].rearrange("p a d -> p (a d)")[:, 0:CH]))
            step(nc.vector.tensor_copy(dst_f[:, :], ps_b[0][:, 1, :, :].rearrange("p a d -> p (a d)")[:, 0:CH]))
            step(nc.vector.tensor_copy(last_f[:, :], ps_b[1][:, 0, :, :].rearrange("p a d -> p (a d)")[:, 0:CH]))
            step(nc.vector.tensor_copy(rel_f[:, :], ps_b[1][:, 1, :, :].rearrange("p a d -> p (a d)")[:, 0:CH]))
            step(nc.vector.tensor_copy(unsorted_i[:, :], ps_m[0:1, 0, 0:1]))
            dve.wait_ge(iota_ok, 2)
            step(nc.vector.tensor_tensor(away, dst_f[:, :], dummy_i, ALU.subtract))
            step(nc.vector.tensor_tensor(away, away, last_f[:, :], ALU.mult))
            step(nc.vector.tensor_tensor(put_i[:, :], away, dummy_i, ALU.add))
            step(nc.vector.tensor_copy(rel_no[:, :], rel_no_i))
            nc.vector.memset(eq_f[:, :], 0.0).then_inc(idx_ok, 1)
            dve.wait_ge(weights_in, 16 * 8)

            def clear_coefficients(l):
                step(nc.vector.memset(coef[l][:, :, :], 0.0))

            def coefficients(l, r, n):
                if not isinstance(r, int) or r:
                    wait(dve, coef_ok, n)
                nc.vector.tensor_scalar(eq_f[:, :], rel_f[:, :], rel_no[:, bass.ds(r, 1)], None,
                                        ALU.is_equal).then_inc(eq_ok, 1)
                dve.wait_ge(eq_ok, n + 1)
                for b in range(NB):
                    i = nc.vector.scalar_tensor_tensor(out=coef[l][:, :, b], in0=eq_f[:, :],
                                                       scalar=w_b[l][:, bass.ds(r * NB + b, 1)],
                                                       in1=coef[l][:, :, b], op0=ALU.mult, op1=ALU.add)
                i.then_inc(coef_ok, 1)

            clear_coefficients(0)
            dve.wait_ge(idx_ok, 1)
            with dve.Fori(0, 1) as r:
                coefficients(0, r, 0)
            with dve.Fori(1, NREL) as r:
                coefficients(0, r, r)
            clear_coefficients(1)
            dve.wait_ge(same_in, 16)

            def messages(s, k, half):
                wait(dve, based, k * 2 + (1 + half))
                if half == 0:
                    wait(dve, coef_set, k + 1)
                    wait(dve, msg_t, k - 1)
                for b in range(half * NB // 2, (half + 1) * NB // 2):
                    for j in range(2):
                        cf = coef_now[:, s, j * NB + b:j * NB + b + 1]
                        o = msg[:, s, j, :]
                        y = ps_b[half][:, j, b % (NB // 2), :]
                        if b == 0:
                            i = nc.vector.tensor_scalar(o, y, cf, None, ALU.mult)
                        else:
                            dve.wait_ge(linked, k * 16 + (2 * b + j - 1))
                            i = nc.vector.scalar_tensor_tensor(out=o, in0=y, scalar=cf, in1=o,
                                                               op0=ALU.mult, op1=ALU.add)
                        i.then_inc(linked, 1)

            def scan(c, s, k, first):
                wait(dve, msg_t, k + 1)
                wait(dve, run_t, k - 1)
                if not first:
                    wait(dve, scanned, k)
                nc.vector.tensor_tensor_scan(run[:, s, :], same[:, bass.ds(c * P, 2 * P)],
                                             ps_m[:, 0:2, :].rearrange("p j e -> p (j e)"),
                                             0.0 if first else run[:, 1 - s, 2 * P - 1:2 * P],
                                             ALU.mult, ALU.add).then_inc(scanned, 1)

            def slow_chunks(l):
                for b in range(NBUF):
                    dve.wait_ge(y_out[b], y_total(b, l))
                dve.wait_ge(slow_mask, 3 * l + 3)
                nc.vector.tensor_copy(slow_row, slow_row_i).then_inc(slow_v, 1)
                with dve.Fori(0, CH) as c:
                    n = c + l * CH
                    col = dst_f[:, bass.ds(c, 1)]
                    v = n * 4 + (l + 1)
                    dve.wait_ge(slow_v, v)
                    nc.vector.tensor_scalar(col_b, ident[:, :], 0.0, col, ALU.mult, ALU.add).then_inc(slow_col, 1)
                    dve.wait_ge(slow_dst, n + 1)
                    nc.vector.tensor_scalar(joins, ps_x[:, 0:P], col, last_f[:, bass.ds(c, 1)],
                                            ALU.is_equal, ALU.mult).then_inc(slow_join, 1)
                    nc.vector.scalar_tensor_tensor(out=after, in0=ps_x[:, 0:P], scalar=col, in1=later_m,
                                                   op0=ALU.is_equal, op1=ALU.mult).then_inc(slow_v, 1)
                    dve.wait_ge(slow_v, v + 1)
                    nc.vector.reduce_max(later, after, axis=AX.X).then_inc(slow_v, 1)
                    nc.vector.tensor_tensor(away_s, slow_row, col, ALU.subtract).then_inc(slow_v, 1)
                    dve.wait_ge(slow_v, v + 3)
                    dve.wait_ge(slow_put, n * 16)
                    nc.vector.scalar_tensor_tensor(out=slow_put_i, in0=later, scalar=away_s, in1=col,
                                                   op0=ALU.mult, op1=ALU.add).then_inc(slow_v, 1)
                    dve.wait_ge(slow_v, v + 4)
                    dve.wait_ge(slow_sum, n + 1)
                    nc.vector.tensor_copy(whole, ps_y[:, 0:D]).then_inc(slow_ready, 1)

            dve_unsorted = dve.value_load(unsorted_i[0:1, 0:1], min_val=0, max_val=E)

            for l in range(2):
                K = l * PAIRS

                def step_m(it, u, m_, c_, K=K):
                    if m_:
                        messages((u + 1) % 2, it * G + (K + u - 1), 0)
                        messages((u + 1) % 2, it * G + (K + u - 1), 1)
                    if c_:
                        scan(it * U + (2 * u - 4), u % 2, it * G + (K + u - 2), isinstance(it, int) and it * G + u == 2)

                for it in range(2):
                    for u in range(G):
                        step_m(it, u, it or u, it)
                if l == 0:
                    with dve.Fori(2, 2 + NREL) as it:
                        for u in range(G):
                            step_m(it, u, True, True)
                        coefficients(1, it - 2, it + (NREL - 2))
                with dve.Fori(2 if l else 2 + NREL, TURNS) as it:
                    for u in range(G):
                        step_m(it, u, True, True)
                step_m(TURNS, 0, True, True)
                step_m(TURNS, 1, False, True)
                with dve.If(dve_unsorted > 0):
                    slow_chunks(l)

            fstat = stage_stats(dve)
            last_vector(dve, fstat)

        @block.scalar
        def _(act):
            act.wait_ge(weights_in, 16 * 8)

            def stage_rows(p, u, k, turn16):
                for j in range(2):
                    wait(act, gathered[(2 * u + j) % U], turn16)
                wait(act, gt_made, k)
                nc.scalar.copy(stage[:, :, :], sums[:, bass.ds(p * 2, 2), :]).then_inc(staged, 1)

            def set_coef(l, p, s, k):
                wait(act, linked, k * 16 - 16)
                nc.scalar.copy(coef_now[:, s, :],
                               coef[l][:, bass.ds(p * 2, 2), :].rearrange("p a b -> p (a b)")).then_inc(coef_set, 1)

            def move_t(l, o, i):
                if l == 0:
                    return nc.scalar.copy(o, i)
                return nc.scalar.activation(o, i, ACT.Relu, bias=bias1_c[:, 0:1])

            def move_run(p, k):
                wait(act, run_t, k + 1)
                nc.scalar.copy(sums[:, bass.ds(p * 2, 2), :], ps_g[:, 2:4, :]).then_inc(summed, 1)

            def move_x(l, h, s, cols=Q * P):
                wait(act, xt_made, h + 1)
                wait(act, y_made, h - 1)
                move_t(l, xT[:, s, 0:cols], ps_x[:, 0:cols]).then_inc(xt_moved, 1)

            def move_y(h, b, j, nj=Q, tail=0):
                wait(act, y_made, h + 1)
                i = nc.scalar.copy(yout[:, b, j:j + nj, :].rearrange("p j d -> p (j d)"), ps_y[:, 0:nj * D])
                if tail:
                    i = nc.scalar.copy(yout[0:tail, b, j + nj, :], ps_y[0:tail, nj * D:(nj + 1) * D])
                i.then_inc(y_moved, 1)

            def coef_ready(l):
                act.wait_ge(coef_ok, NREL * (l + 1))

            for l in range(2):
                K = l * PAIRS
                H = l * HALVES

                def step_m(it, u, next_, a_, d_, dense, l=l, K=K, H=H):
                    p = it * G + u
                    k = it * G + (K + u)
                    if a_:
                        wait(act, gt_made, k + 1)
                        if d_:
                            wait(act, run_t, k - (LAG - 1))
                        wait(act, based, k * 2 - 2)
                        move_t(l, gT[:, u % 2, :, :], ps_g[:, 0:2, :]).then_inc(gt_moved, 1)
                    if d_:
                        move_run(it * G + (u - LAG), k - LAG)
                    if a_:
                        set_coef(l, p, u % 2, k)
                    h = it * (2 * G) + (H + 2 * u)
                    if dense:
                        move_x(l, h, 0)
                        if not (isinstance(it, int) and it == 0 and u == 0):
                            move_y(h - 1, (u + 1) % 2, Q)
                    if next_:
                        it_ = it if u + 1 < G else it + 1
                        stage_rows(it * G + (u + 1), (u + 1) % G, k + 1, it_ * 16 + (16 + 16 * l * TURNS))
                    if dense:
                        move_x(l, h + 1, 1)
                        wait(act, y_out[u], it * 16 + (y_total(u, 0) if l else 0))
                        move_y(h, u % 2, 0)

                stage_rows(0, 0, K, 16 + 16 * l * TURNS)
                coef_ready(l)
                for it in range(2):
                    for u in range(G):
                        step_m(it, u, True, True, False, True)
                with act.Fori(2, DTURNS) as it:
                    for u in range(G):
                        step_m(it, u, True, True, True, True)
                h = H + 2 * NBLK
                move_x(l, h, 0)
                move_y(h - 1, 1, Q)
                move_x(l, h + 1, 1, (TAILQ - Q) * P + TAIL)
                act.wait_ge(y_out[0], y_total(0, l) - 32)
                move_y(h, 0, 0)
                move_y(h + 1, 0, Q, TAILQ - Q, TAIL)
                with act.Fori(DTURNS, TURNS - 1) as it:
                    for u in range(G):
                        step_m(it, u, True, True, True, False)
                for u in range(G):
                    step_m(TURNS - 1, u, u < G - 1, True, True, False)
                for m in range(LAG):
                    step_m(TURNS + m // G, m % G, False, False, True, False)

            f = stage_stats(None)

            def one(k, b, rows=P, nj=FJ):
                h, xx = final_tiles(b)
                act.wait_ge(f_var, k * 4 + 3)
                nc.scalar.activation(f["q"][b][0:rows, 0:nj], f["v"][b][0:rows, 0:nj], ACT.Sqrt).then_inc(f_std, 1)
                act.wait_ge(f_norm, k + 1)
                for j in range(nj):
                    i = nc.scalar.activation(xx[0:rows, j, :], h[0:rows, j, :], ACT.Identity,
                                             bias=f["o"][b][0:rows, j:j + 1], scale=f["r"][b][0:rows, j:j + 1])
                i.then_inc(f_done, 1)

            with act.Fori(0, FN // FBUF) as r:
                for b in range(FBUF):
                    one(r * FBUF + b, b)
            one(FN, 0, TAIL, 1)

        @block.tensor
        def _(pe):
            pe.wait_ge(ident_ok, 2)
            pe.wait_ge(vdone, 12)
            pe.wait_ge(vdone, 12)
            homes = {"src": (0, 0), "dst": (0, 1), "last": (1, 0), "rel": (1, 1)}
            for k, (s, a) in homes.items():
                o = ps_b[s][:, a, :, :].rearrange("p a d -> p (a d)")
                nc.tensor.transpose(o[:, 0:P], val[k][:, 0, :], ident[:, :])
                nc.tensor.transpose(o[:, P:CH], val[k][0:CH - P, 1, :], ident[0:CH - P, 0:CH - P])
            nc.tensor.matmul(ps_m[0:1, 0, 0:1], ones_c, worst, start=True, stop=True).then_inc(setup_t, 1)
            pe.wait_ge(weights_in, 16 * 8)
            pe.wait_ge(idx_ok, 1)
            pe_unsorted = pe.value_load(unsorted_i[0:1, 0:1], min_val=0, max_val=E)

            def slow_chunks(l):
                pe.wait_ge(summed, PAIRS * (l + 1))
                with pe.Fori(0, CH) as c:
                    pe.wait_ge(slow_col, c + (l * CH + 1))
                    nc.tensor.matmul(ps_x[:, 0:P], col_b, ident[:, :], start=True, stop=True).then_inc(slow_dst, 1)
                    pe.wait_ge(slow_join, c + (l * CH + 1))
                    nc.tensor.matmul(ps_y[:, 0:D], joins, sums[:, bass.ds(c, 1), :].rearrange("p a d -> p (a d)"),
                                     start=True, stop=True).then_inc(slow_sum, 1)

            for l in range(2):
                K = l * PAIRS
                H = l * HALVES
                bl = basis[l][:, :, :].rearrange("p b d -> p (b d)")

                def node_t(h, s, b, j, tiles=Q, tail=0, x_count=None, l=l):
                    if x_count is not None:
                        pe.wait_ge(x_in[b], x_count)
                    wait(pe, xt_moved, h)
                    for q in range(tiles):
                        i = nc.tensor.transpose(ps_x[:, q * P:(q + 1) * P], xin[:, b, j + q, :], ident[:, :])
                    if tail:
                        i = nc.tensor.transpose(ps_x[:, tiles * P:tiles * P + tail], xin[0:tail, b, j + tiles, :],
                                                ident[0:tail, 0:tail])
                    i.then_inc(xt_made, 1)

                def node_mm(h, s, tiles=Q, tail=0, l=l):
                    wait(pe, xt_moved, h + 1)
                    wait(pe, y_moved, h)
                    for q in range(tiles):
                        i = nc.tensor.matmul(ps_y[:, q * D:(q + 1) * D], xT[:, s, q * P:(q + 1) * P],
                                             loop_w[l][:, :], start=True, stop=True)
                    if tail:
                        i = nc.tensor.matmul(ps_y[0:tail, tiles * D:(tiles + 1) * D],
                                             xT[:, s, tiles * P:tiles * P + tail],
                                             loop_w[l][:, :], start=True, stop=True)
                    i.then_inc(y_made, 1)

                def times_bases(k, s, half, bl=bl):
                    wait(pe, linked, k * 16 - (8 if half == 0 else 0))
                    w = NB // 2 * D
                    for j in range(2):
                        i = nc.tensor.matmul(ps_b[half][:, j, :, :].rearrange("p b d -> p (b d)"), gT[:, s, j, :],
                                             bl[:, half * w:(half + 1) * w], start=True, stop=True)
                    i.then_inc(based, 1)

                def step_m(it, u, a_, b_, c_, d_, dense, l=l, K=K, H=H):
                    k = it * G + (K + u)
                    s = u % 2
                    if b_:
                        wait(pe, gt_moved, k)
                        times_bases(k - 1, 1 - s, 0)
                    wait(pe, gt_moved, k if a_ or b_ else K + PAIRS)
                    wait(pe, summed, k - LAG if d_ else (K if l else 0))
                    if a_:
                        wait(pe, staged, k + 1)
                        for j in range(2):
                            i = nc.tensor.transpose(ps_g[:, j, :], stage[:, j, :], ident[:, :])
                        i.then_inc(gt_made, 1)
                    if d_:
                        wait(pe, scanned, k - (LAG - 1))
                        for j in range(2):
                            i = nc.tensor.transpose(ps_g[:, 2 + j, :], run[:, s, j * P:(j + 1) * P], ident[:, :])
                        i.then_inc(run_t, 1)
                    h = it * (2 * G) + (H + 2 * u)
                    if dense:
                        node_t(h, 0, u, 0, x_count=it * 16 + (16 + (y_total(u, 0) if l else 0)))
                        if not (isinstance(it, int) and it == 0 and u == 0):
                            node_mm(h - 1, 1)
                    if b_:
                        times_bases(k - 1, 1 - s, 1)
                    if c_:
                        wait(pe, linked, k * 16 - 16)
                        wait(pe, scanned, k - 2)
                        for j in range(2):
                            i = nc.tensor.transpose(ps_m[:, j, :], msg[:, s, j, :], ident[:, :])
                        i.then_inc(msg_t, 1)
                    if dense:
                        node_t(h + 1, 1, u, Q)
                        node_mm(h, 0)

                for it in range(2):
                    for u in range(G):
                        step_m(it, u, True, it or u, it, False, True)
                with pe.Fori(2, DTURNS) as it:
                    for u in range(G):
                        step_m(it, u, True, True, True, True, True)
                h = H + 2 * NBLK
                node_t(h, 0, 0, 0, x_count=y_total(0, l))
                node_mm(h - 1, 1)
                node_t(h + 1, 1, 0, Q, TAILQ - Q, TAIL)
                node_mm(h, 0)
                node_mm(h + 1, 1, TAILQ - Q, TAIL)
                with pe.Fori(DTURNS, TURNS) as it:
                    for u in range(G):
                        step_m(it, u, True, True, True, True, False)
                for m in range(LAG):
                    step_m(TURNS + m // G, m % G, False, m < 1, m < 2, True, False)
                with pe.If(pe_unsorted > 0):
                    slow_chunks(l)


_INS = ['x', 'src', 'dst', 'edge_type_16', 'L0_gnn_basis1', 'L0_gnn_w_comp1', 'L0_gnn_loop_w1', 'L0_gnn_bias1',
        'L0_gnn_basis2', 'L0_gnn_w_comp2', 'L0_gnn_loop_w2', 'L0_gnn_bias2']


def kernel(**inputs):
    import numpy as _np
    import concourse.bacc as _bacc
    from concourse import mybir as _mybir
    from concourse.bass_utils import run_bass_kernel_spmd as _run

    nc = _bacc.Bacc("TRN2", target_bir_lowering=False, num_devices=1)
    arrays, args = {}, []
    for name in _INS:
        a = _np.ascontiguousarray(inputs[name])
        arrays[f"in_{name}"] = a
        args.append(nc.dram_tensor(f"in_{name}", a.shape, _mybir.dt.from_np(a.dtype), kind="ExternalInput").ap())
    args.append(nc.dram_tensor("out_rows", (N, D), _mybir.dt.float32, kind="ExternalOutput").ap())
    build_rgcn(nc, *args)
    r = _run(nc, [arrays], core_ids=[0])
    return r.results[0]["out_rows"]
```

```python
from contextlib import ExitStack

import concourse.bass as bass
from concourse import mybir

F32 = mybir.dt.float32
F32R = mybir.dt.float32r
BF16 = mybir.dt.bfloat16
I32 = mybir.dt.int32
ALU = mybir.AluOpType
ACT = mybir.ActivationFunctionType
AX = mybir.AxisListType

P = 128
N = 50000
E = 25000
D = 128
NREL = 16
NB = 8

CH = -(-E // P)
U = 4
G = 2
PAIRS = CH // 2
TURNS = PAIRS // G
LAG = 4
FULL = E // P
REST = E - FULL * P
HALF1 = FULL - P

J = 8
Q = 4
BLK = J * P
NBLK = N // BLK
TAILQ = (N - NBLK * BLK) // P
TAIL = N - NBLK * BLK - TAILQ * P
NBUF = 2
DTURNS = NBLK // G
DFIRST = (5, 0)
MIXED = tuple(DTURNS - d for d in DFIRST)
HALVES = 2 * NBLK + 2

PARTS = 3
MG = 32
MARKS = -(-CH // MG)
CG = 4 * P // (PARTS * 2 * NB)
GROUPS = -(-CH // CG)
SAME_PARTS = ((0, 16, 8, 0), (16, 52, 20, 1), (52, U * (MIXED[0] + 1), 32, 1),
              (U * (MIXED[0] + 1), 124, 56, 2), (124, 160, 72, 2), (160, CH, 88, 2))

SC = 14
DUMMY = N
SLOW = DUMMY + SC * P
ROWS = SLOW + P

FJ = 10
FBLK = FJ * P
FN = N // FBLK
FTAIL = N - FN * FBLK
FBUF = 7
XTURNS = 3
XBUF = XTURNS * FBUF
XSAME = CH * P // 2 // (FJ * D)
FTURNS = FN // FBUF
XLEAD = 16
EPS = 1e-5


def build_rgcn(nc, x, src, dst, rel, basis1, w_comp1, loop_w1, bias1,
               basis2, w_comp2, loop_w2, bias2, out):
    ctx = ExitStack()
    with ctx:
        def sb(name, shape, dt=F32):
            return ctx.enter_context(nc.sbuf_tensor(name, shape, dt))

        def ps(name, shape):
            return ctx.enter_context(nc.psum_tensor(name, shape, F32))

        def sem(name):
            return ctx.enter_context(nc.semaphore(name))

        nodes = [nc.dram_tensor(f"nodes{l}", (ROWS, D), F32).ap() for l in range(2)]
        rel_d = nc.dram_tensor("rel_d", (CH * P,), BF16).ap()
        same_d = nc.dram_tensor("same_d", (CH * P,), BF16).ap()

        store = sb("store", [P, CH * P // 2 + CH * D])
        same = store[:, 0:CH * P // 2].bitcast(BF16)
        sums = store[:, CH * P // 2:].rearrange("p (c d) -> p c d", d=D)
        coef_all = sb("coef_all", [P, CH, 2 * NB])
        coef = [coef_all[:, :, l * NB:(l + 1) * NB] for l in range(2)]
        src_i = sb("src_i", [P, CH], I32)
        coef_now = sb("coef_now", [P, 2, 2 * NB])
        put_i = sb("put_i", [P, CH], I32)
        dst_f = sb("dst_f", [P, CH])
        last_f = sb("last_f", [P, CH])
        basis_hi = sb("basis_hi", [P, NB * D], F32R)
        basis_lo = sb("basis_lo", [P, NB * D], F32R)
        loop_w = [sb(f"loop_w{l}", [P, D]) for l in range(2)]
        ident = sb("ident", [P, P])
        bias1_c = sb("bias1_c", [P, 1])
        bias2_b = sb("bias2_b", [P, D])
        w_in = sb("w_in", [NREL, 2 * NB])
        w_rest = sb("w_rest", [NREL, 2, 2 * NB])
        w_parts = sb("w_parts", [NREL, PARTS, 2 * NB], BF16)
        rel_no = sb("rel_no", [NREL, 1])
        unsorted_i = sb("unsorted_i", [1, 1], I32)
        xin = sb("xin", [P, NBUF, J, D])
        yout = sb("yout", [P, NBUF, J, D])
        stage = sb("stage", [P, 2, D])
        gT = sb("gT", [P, 2, 2, P])
        gT_hi = sb("gT_hi", [P, 2, 2, P], F32R)
        gT_lo = sb("gT_lo", [P, 2, 2, P], F32R)
        msg = sb("msg", [P, 2, 2, D])
        run = sb("run", [P, 2, 2 * P])
        xT = sb("xT", [P, 2, Q * P])

        def scratch(first, chunks):
            return sums[:, first:first + chunks, :]
        raw = {k: scratch(CH - 20 + 2 * i, 2).bitcast(I32) for i, k in enumerate(("src", "dst", "nxt", "prv", "rel"))}
        val = {k: scratch(CH - 10 + 2 * i, 2) for i, k in enumerate(("src", "dst", "last"))}
        bigger = scratch(CH - 2, 2)
        dummy_i = sums[:, CH - 22:CH - 20, :].rearrange("p a d -> p (a d)")[:, 0:CH].bitcast(I32)
        away = sums[:, CH - 24:CH - 22, :].rearrange("p a d -> p (a d)")[:, 0:CH]
        same_h = sums[:, CH - 25, :].bitcast(BF16).rearrange("p (a d) -> p a d", a=2)
        zeros = scratch(CH - 40, SC + 1)
        rel_no_i = sums[0:NREL, CH - 46, 32:33].bitcast(I32)
        rel_h = sums[:, CH - 44, :].bitcast(BF16).rearrange("p (a d) -> p a d", a=2)
        rel_b = sums[0:NREL, CH - 54 - CH // 2:CH - 54, :].rearrange("p c d -> p (c d)").bitcast(BF16)
        ones_c = sums[:, CH - 46, 64:65]
        worst = sums[:, CH - 46, 65:66]

        basis_raw = scratch(CH - 54, NB)
        share = yout[:, 1, :, :].rearrange("p (s h j) d -> p s h j d", s=2, h=2)

        col_b = xin[:, 0, 0, :]
        joins = xin[:, 0, 1, :]
        after = xin[:, 0, 2, :]
        later_m = xin[:, 0, 3, :]
        slow_row = xin[:, 0, 4, 0:1]
        later = xin[:, 0, 4, 1:2]
        away_s = xin[:, 0, 4, 2:3]
        slow_row_i = xin[:, 0, 4, 3:4].bitcast(I32)
        slow_put_i = yout[:, 0, 0, 0:1].bitcast(I32)
        whole = yout[:, 0, 1, :]

        ps_g = ps("ps_g", [P, 4, P])
        ps_m = ps("ps_m", [P, 4, P])
        ps_x = ps("ps_x", [P, Q * P])
        ps_y = ps("ps_y", [P, Q * D])
        ps_b = [ps(f"ps_b{h}", [P, 2, NB // 2, D]) for h in range(2)]


        def coef_bank(g):
            return ps_b[g % 4 // 2][:, g % 2, :, :].rearrange("p b d -> p (b d)")

        cleared = sem("cleared")
        idx_in = sem("idx_in")
        weights_in = sem("weights_in")
        basis_room = sem("basis_room")
        basis_in = sem("basis_in")
        basis_top = sem("basis_top")
        basis_ok = sem("basis_ok")
        ident_ok = sem("ident_ok")
        iota_ok = sem("iota_ok")
        vdone = sem("vdone")
        setup_t = sem("setup_t")
        idx_ok = sem("idx_ok")
        rel_in = sem("rel_in")
        marks_ok = sem("marks_ok")
        rel_w = sem("rel_w")
        rel_back = sem("rel_back")
        comp_in = sem("comp_in")
        w_done = sem("w_done")
        onehot = sem("onehot")
        coef_made = sem("coef_made")
        coef_ok = sem("coef_ok")
        loop_in = sem("loop_in")
        same_w = sem("same_w")
        same_in = [sem(f"same_in{i}") for i in range(3)]
        zero_w = sem("zero_w")
        gathered = [sem(f"gathered{u}") for u in range(U)]
        staged = sem("staged")
        coef_set = sem("coef_set")
        gt_made = sem("gt_made")
        gt_moved = sem("gt_moved")
        gt_rest = sem("gt_rest")
        shared = sem("shared")
        based = sem("based")
        linked = sem("linked")
        msg_t = sem("msg_t")
        scanned = sem("scanned")
        run_t = sem("run_t")
        summed = sem("summed")
        x_in = [sem(f"x_in{b}") for b in range(NBUF)]
        xt_made = sem("xt_made")
        xt_moved = sem("xt_moved")
        y_made = sem("y_made")
        y_moved = sem("y_moved")
        y_out = [sem(f"y_out{b}") for b in range(NBUF)]
        put = [sem(f"put{u}") for u in range(SC)]
        slow_mask = sem("slow_mask")
        slow_col = sem("slow_col")
        slow_dst = sem("slow_dst")
        slow_join = sem("slow_join")
        slow_sum = sem("slow_sum")
        slow_v = sem("slow_v")
        slow_ready = sem("slow_ready")
        slow_put = sem("slow_put")
        layer_put = sem("layer_put")
        x_room = sem("x_room")
        f_in = [sem(f"f_in{b}") for b in range(FBUF)]
        x_early = sem("x_early")
        fx_in = [sem(f"fx_in{b}") for b in range(FBUF)]
        f_bias = sem("f_bias")
        f_sum = sem("f_sum")
        f_stat = sem("f_stat")
        f_var = sem("f_var")
        f_std = sem("f_std")
        f_norm = sem("f_norm")
        f_done = sem("f_done")
        f_out = [sem(f"f_out{b}") for b in range(FBUF)]


        def y_total(b, l):
            return 16 * (NBLK // NBUF + 2 * (b == 0)) * (l + 1)

        def unshared(l):
            return 2 * sum(G * m for m in MIXED[:l + 1])

        def put_total(u, l):
            return 16 * (l + 1) * (CH // SC)

        def node_block(k, l):
            t = x if l == 0 else nodes[0]
            return t[bass.ds(k * BLK, BLK), :].rearrange("(p j) d -> p j d", j=J)

        def wait(eng, s, v):
            if not isinstance(v, int) or v > 0:
                eng.wait_ge(s, v)

        def f_rows(k):
            lo = XBUF * FJ - CH // 2 + FJ * (k % FBUF)
            return sums[:, lo:lo + FJ, :]

        def f_x(slot):
            return store[:, bass.ds(slot * (FJ * D), FJ * D)].rearrange("p (j d) -> p j d", d=D)

        def scattered(slot):
            return FJ * (slot + 1) - CH // 2

        def f_small(k):
            base = (XBUF + FBUF) * FJ - CH // 2 + k % FBUF
            f = {"bn": sums[:, base, 0:6 * FJ].rearrange("p (j s) -> p j s", s=6)}
            for i, name in enumerate("sdqvro"):
                f[name] = sums[:, base + FBUF, i * 16:i * 16 + FJ]
            return f

        def f_block(t, k):
            return t[bass.ds(k * FBLK, FBLK), :].rearrange("(p j) d -> p j d", j=FJ)

        block = ctx.enter_context(nc.Block())

        @block.sync
        def _(sp):
            def load_edges(tile, a, shift, s=idx_in):
                cut = P * P + shift
                if shift < 0:
                    sp.dma_start(tile[0:1, 0, 1:P], a[0:P - 1].rearrange("(p j) -> p j", p=1)).then_inc(s, 16)
                    sp.dma_start(tile[1:P, 0, :], a[P - 1:cut].rearrange("(p j) -> p j", j=P)).then_inc(s, 16)
                else:
                    sp.dma_start(tile[:, 0, :], a[shift:cut].rearrange("(p j) -> p j", j=P)).then_inc(s, 16)
                end = cut + HALF1 * P
                left = min(REST, E - end)
                sp.dma_start(tile[0:HALF1, 1, :], a[cut:end].rearrange("(p j) -> p j", j=P)).then_inc(s, 16)
                sp.dma_start(tile[HALF1:HALF1 + 1, 1, 0:left],
                             a[end:end + left].rearrange("(p j) -> p j", p=1)).then_inc(s, 16)

            sp.dma_start(xin[:, 0, :, :], node_block(0, 0)).then_inc(x_in[0], 16)
            sp.dma_start(loop_w[0][:, :], loop_w1).then_inc(loop_in, 16)
            sp.dma_start(xin[:, 1, :, :], node_block(1, 0)).then_inc(x_in[1], 16)
            sp.wait_ge(cleared, 1)
            load_edges(raw["rel"], rel, 0, rel_in)
            load_edges(raw["src"], src, 0)
            load_edges(raw["dst"], dst, 0)
            load_edges(raw["nxt"], dst, 1)
            load_edges(raw["prv"], dst, -1)
            sp.dma_start(w_in[:, 0:NB], w_comp1).then_inc(comp_in, 16)
            sp.dma_start(w_in[:, NB:2 * NB], w_comp2).then_inc(comp_in, 16)

            for l in range(2):
                if l == 1:
                    sp.wait_ge(basis_room, 1)
                    sp.dma_start(basis_raw, basis2.rearrange("b i o -> i b o")).then_inc(basis_in, 16)
                    sp.wait_ge(layer_put, 1)
                    for b in range(NBUF):
                        sp.dma_start(xin[:, b, :, :], node_block(b, l)).then_inc(x_in[b], 16)
                h0 = l * HALVES

                def move_block(k, b, more):
                    if more:
                        sp.wait_ge(xt_made, k * 2 + (h0 + 2))
                        sp.dma_start(xin[:, b, :, :], node_block(k + NBUF, l)).then_inc(x_in[b], 16)
                    sp.wait_ge(y_moved, k * 2 + (h0 + 2))
                    sp.dma_start(nodes[l][bass.ds(k * BLK, BLK), :].rearrange("(p j) d -> p j d", j=J),
                                 yout[:, b, :, :]).then_inc(y_out[b], 16)

                with sp.Fori(0, NBLK // NBUF - 1) as r:
                    for b in range(NBUF):
                        move_block(r * NBUF + b, b, True)
                t = x if l == 0 else nodes[0]
                lo = NBLK * BLK
                mid = lo + TAILQ * P
                sp.wait_ge(xt_made, h0 + 2 * (NBLK - 1))
                sp.dma_start(xin[:, 0, 0:TAILQ, :], t[lo:mid, :].rearrange("(p j) d -> p j d", j=TAILQ)).then_inc(x_in[0], 16)
                sp.dma_start(xin[0:TAIL, 0, TAILQ, :], t[mid:N, :]).then_inc(x_in[0], 16)
                for b in range(NBUF):
                    move_block(NBLK - NBUF + b, b, False)
                sp.wait_ge(y_moved, h0 + HALVES)
                sp.dma_start(nodes[l][lo:mid, :].rearrange("(p j) d -> p j d", j=TAILQ),
                             yout[:, 0, 0:TAILQ, :]).then_inc(y_out[0], 16)
                sp.dma_start(nodes[l][mid:N, :], yout[0:TAIL, 0, TAILQ, :]).then_inc(y_out[0], 16)

            def load_x(k, done):
                if k < FN:
                    sp.dma_start(f_x(k % XBUF), f_block(x, k)).then_inc(done, 16)
                elif k == FN:
                    sp.dma_start(f_x(k % XBUF)[0:FTAIL, 0, :], x[N - FTAIL:N, :]).then_inc(done, 16)

            def load_rows(k):
                if k < FN:
                    sp.dma_start(f_rows(k), f_block(nodes[1], k)).then_inc(f_in[k % FBUF], 16)
                elif k == FN:
                    sp.dma_start(f_rows(k)[0:FTAIL, 0, :], nodes[1][N - FTAIL:N, :]).then_inc(f_in[k % FBUF], 16)

            def load_marked(k):
                sp.wait_ge(scanned, PAIRS + min(-(-FJ * (k + 1) // 2) * 2, PAIRS))
                load_x(k, x_early)

            half = XSAME // 2
            for k in range(half):
                load_marked(k)
            for k in range(XSAME + 1, XBUF):
                sp.wait_ge(x_room, k - XSAME + 1)
                load_x(k, x_early)
            for k in range(half, XSAME + 1):
                load_marked(k)
            sp.wait_ge(layer_put, 2)
            for k in range(FBUF):
                load_rows(k)
            for k in range(FN):
                if k >= FBUF:
                    sp.wait_ge(f_out[k % FBUF], 16 * (k // FBUF))
                sp.wait_ge(f_done, k + 1)
                sp.dma_start(f_block(out, k), f_x(k % XBUF)).then_inc(f_out[k % FBUF], 16)
                load_rows(k + FBUF)
                new = k + XLEAD
                if XBUF <= new <= FN:
                    old = new - XBUF
                    sp.wait_ge(f_out[old % FBUF], 16 * (old // FBUF + 1))
                    if new >= XBUF + FBUF:
                        sp.wait_ge(fx_in[new % FBUF], 16 * (new // FBUF - XTURNS))
                    load_x(new, fx_in[new % FBUF])
            sp.wait_ge(f_done, FN + 1)
            sp.dma_start(out[N - FTAIL:N, :], f_x(FN % XBUF)[0:FTAIL, 0, :]).then_inc(f_out[FN % FBUF], 16)
            for b in range(FBUF):
                sp.wait_ge(f_out[b], 16 * len(range(b, FN + 1, FBUF)))

        @block.gpsimd
        def _(pool):
            limit = pool.snap(pool.to_reg(ROWS - 1))
            pool.memset(ident[:, :], 0.0).then_inc(ident_ok, 1)
            pool.wait_ge(ident_ok, 1)
            pool.affine_select(out=ident[:, :], in_=ident[:, :], compare_op=ALU.not_equal, fill=1.0,
                               base=0, pattern=[[-1, P]], channel_multiplier=1).then_inc(ident_ok, 1)
            pool.iota(dummy_i, pattern=[[0, CH // SC], [P, SC]], base=DUMMY, channel_multiplier=1).then_inc(iota_ok, 1)
            pool.wait_ge(iota_ok, 1)
            pool.iota(rel_no_i, pattern=[[0, 1]], base=0, channel_multiplier=1).then_inc(iota_ok, 1)
            pool.wait_ge(marks_ok, 1)
            pool.dma_start(rel_d[0:P * P].rearrange("(p j) -> p j", j=P), rel_h[:, 0, :]).then_inc(rel_w, 16)
            pool.dma_start(rel_d[P * P:CH * P].rearrange("(p j) -> p j", j=P), rel_h[0:CH - P, 1, :]).then_inc(rel_w, 16)
            pool.wait_ge(rel_w, 32)
            pool.dma_start(rel_b[:, :], rel_d.partition_broadcast(NREL)).then_inc(rel_back, 16)
            pool.wait_ge(marks_ok, 2)
            pool.dma_start(same_d[0:P * P].rearrange("(p j) -> p j", j=P), same_h[:, 0, :]).then_inc(same_w, 16)
            pool.dma_start(same_d[P * P:CH * P].rearrange("(p j) -> p j", j=P), same_h[0:CH - P, 1, :]).then_inc(same_w, 16)
            pool.wait_ge(idx_ok, 1)
            unsorted = pool.value_load(unsorted_i[0:1, 0:1], min_val=0, max_val=E)

            def slow_scatters(l):
                pool.iota(slow_row_i, pattern=[[0, 1]], base=SLOW, channel_multiplier=1).then_inc(slow_mask, 1)
                pool.memset(later_m, 1.0).then_inc(slow_mask, 1)
                pool.wait_ge(slow_mask, 3 * l + 2)
                pool.affine_select(out=later_m, in_=later_m, compare_op=ALU.is_gt, fill=0.0, base=0,
                                   pattern=[[1, P]], channel_multiplier=-1).then_inc(slow_mask, 1)
                with pool.Fori(l * CH + 1, l * CH + CH + 1) as n:
                    pool.wait_ge(slow_ready, n)
                    pool.nop(nofuse=True)
                    pool.indirect_dma_start(
                        out=nodes[l][:, :], out_offset=bass.IndirectOffsetOnAxis(ap=slow_put_i, axis=0),
                        in_=whole, in_offset=None, bounds_check=limit, oob_is_err=True,
                        compute_op=ALU.add).then_inc(slow_put, 16)
                    done = pool.snap(n * 16)
                    pool.wait_ge(slow_put, done)
                    pool.nop(nofuse=True)

            def scatter(l, c):
                if c % 2 == 0:
                    pool.wait_ge(summed, l * PAIRS + c // 2 + 1)
                if l * CH + c >= SC:
                    pool.wait_ge(put[c % SC], 16 * (l * (CH // SC) + c // SC))
                    if l == 0 and c - SC + 1 == CH - 54 + NB:
                        pool.sem_inc(basis_room, 1)
                    if l == 1 and c - SC + 1 in [scattered(k) for k in range(XSAME, XBUF)]:
                        pool.sem_inc(x_room, 1)
                pool.indirect_dma_start(
                    out=nodes[l][:, :], out_offset=bass.IndirectOffsetOnAxis(ap=put_i[:, c:c + 1], axis=0),
                    in_=sums[:, c, :], in_offset=None, bounds_check=limit, oob_is_err=True,
                    compute_op=ALU.add).then_inc(put[c % SC], 16)

            for l in range(2):
                table = x if l == 0 else nodes[0]
                for c in range(CH):
                    for c0, c1, at, i in SAME_PARTS:
                        if l == 0 and c == at:
                            if i == 0:
                                pool.wait_ge(same_w, 32)
                            e = slice(c0 * P, c1 * P)
                            pool.dma_start(same[:, e], same_d[e].partition_broadcast(P)).then_inc(same_in[i], 16)
                    if l == 0 and c == CH - 54 - CH // 2:
                        pool.wait_ge(coef_made, GROUPS)
                    if c == CH - 54:
                        pool.wait_ge(basis_ok, l + 1)
                    if l == 0 and c == CH - 54:
                        pool.wait_ge(idx_ok, 1)
                        pool.wait_ge(zero_w, 32)
                        pool.wait_ge(same_w, 32)
                        pool.wait_ge(setup_t, 1)
                    if l * CH + c >= U:
                        turn = l * TURNS + c // U
                        pool.wait_ge(gathered[c % U], 16 * turn)
                    pool.indirect_dma_start(
                        out=sums[:, c, :], out_offset=None, in_=table[:, :],
                        in_offset=bass.IndirectOffsetOnAxis(ap=src_i[:, c:c + 1], axis=0)).then_inc(gathered[c % U], 16)
                for b in range(NBUF):
                    pool.wait_ge(y_out[b], y_total(b, l))
                with pool.If(unsorted < 1):
                    for c in range(CH):
                        scatter(l, c)
                    for u in range(SC):
                        pool.wait_ge(put[u], put_total(u, l))
                with pool.If(unsorted > 0):
                    slow_scatters(l)
                    if l == 0:
                        pool.sem_inc(basis_room, 1)
                    else:
                        pool.sem_inc(x_room, XBUF - XSAME)
                pool.sem_inc(layer_put, 1)

            pool.wait_ge(weights_in, 16 * 3)

            def add_bias(turn, j, rows=P, nj=FJ):
                h = f_rows(j)[0:rows, 0:nj, :]
                pool.wait_ge(f_in[j], turn * 16 + 16)
                nc.gpsimd.tensor_tensor(h, h, bias2_b[0:rows, :].unsqueeze(1).to_broadcast([rows, nj, D]),
                                        ALU.add).then_inc(f_bias, 1)

            with pool.Fori(0, FTURNS) as t:
                for j in range(FBUF):
                    add_bias(t, j)
            for j in range(FN % FBUF):
                add_bias(FTURNS, j)
            add_bias(FTURNS, FN % FBUF, FTAIL, 1)

        @block.vector
        def _(dve):
            steps = [0]

            def step(ins):
                steps[0] += 1
                ins.then_inc(vdone, 1)
                dve.wait_ge(vdone, steps[0])

            step(nc.vector.memset(raw["src"], 0))
            step(nc.vector.memset(raw["dst"], DUMMY))
            step(nc.vector.memset(raw["nxt"], DUMMY))
            step(nc.vector.memset(raw["prv"], -1))
            step(nc.vector.memset(zeros, 0.0))
            step(nc.vector.memset(ones_c, 1.0))
            nc.vector.memset(raw["rel"], 0).then_inc(cleared, 1)
            dve.wait_ge(rel_in, 3 * 16)
            nc.vector.tensor_copy(rel_h, raw["rel"]).then_inc(marks_ok, 1)
            dve.wait_ge(idx_in, 13 * 16)
            step(nc.vector.tensor_copy(val["src"], raw["src"]))
            step(nc.vector.tensor_copy(val["dst"], raw["dst"]))
            step(nc.vector.tensor_tensor(val["last"], raw["dst"], raw["nxt"], ALU.not_equal))
            nc.vector.tensor_tensor(same_h, raw["dst"], raw["prv"], ALU.is_equal).then_inc(marks_ok, 1)
            step(nc.vector.tensor_tensor(bigger, raw["dst"], raw["nxt"], ALU.is_gt))
            step(nc.vector.reduce_sum(worst, bigger.rearrange("p a d -> p (a d)"), axis=AX.X))
            dve.wait_ge(setup_t, 1)
            step(nc.vector.tensor_copy(src_i[:, :], ps_b[0][:, 0, :, :].rearrange("p a d -> p (a d)")[:, 0:CH]))
            step(nc.vector.tensor_copy(dst_f[:, :], ps_b[0][:, 1, :, :].rearrange("p a d -> p (a d)")[:, 0:CH]))
            step(nc.vector.tensor_copy(last_f[:, :], ps_b[1][:, 0, :, :].rearrange("p a d -> p (a d)")[:, 0:CH]))
            step(nc.vector.tensor_copy(unsorted_i[:, :], ps_m[0:1, 0, 0:1]))
            dve.wait_ge(iota_ok, 2)
            step(nc.vector.tensor_tensor(away, dst_f[:, :], dummy_i, ALU.subtract))
            step(nc.vector.tensor_tensor(away, away, last_f[:, :], ALU.mult))
            step(nc.vector.tensor_tensor(put_i[:, :], away, dummy_i, ALU.add))
            nc.vector.tensor_copy(rel_no[:, :], rel_no_i).then_inc(idx_ok, 1)

            def split_basis(l):
                dve.wait_ge(basis_top, l + 1)
                if l:
                    dve.wait_ge(based, 2 * PAIRS)
                nc.vector.tensor_tensor(basis_lo[:, :], basis_raw.rearrange("p b d -> p (b d)"),
                                        basis_hi[:, :].bitcast(F32), ALU.subtract).then_inc(basis_ok, 1)

            def mark(m):
                r = rel_b[:, m * MG * P:min((m + 1) * MG, CH) * P]
                nc.vector.tensor_scalar(r, r, rel_no[:, 0:1], None, ALU.is_equal).then_inc(onehot, 1)

            def keep(g):
                dve.wait_ge(coef_made, g + 1)
                c = slice(g * CG, min((g + 1) * CG, CH))
                n = (c.stop - c.start) * PARTS * 2 * NB
                part = coef_bank(g)[:, 0:n].rearrange("p (c i b) -> p c b i", i=PARTS, b=2 * NB)
                nc.vector.tensor_reduce(out=coef_all[:, c, :], in_=part, axis=AX.X, op=ALU.add).then_inc(coef_ok, 1)

            dve.wait_ge(idx_ok, 1)
            dve.wait_ge(rel_back, 16)
            mark(0)
            mark(1)
            dve.wait_ge(comp_in, 16 * 2)
            left = [w_in[:, :], w_rest[:, 0, :], w_rest[:, 1, :]]
            for i in range(PARTS):
                nc.vector.tensor_copy(w_parts[:, i, :], left[i]).then_inc(w_done, 1)
                if i + 1 < PARTS:
                    dve.wait_ge(w_done, 2 * i + 1)
                    nc.vector.tensor_tensor(left[i + 1], left[i], w_parts[:, i, :], ALU.subtract).then_inc(w_done, 1)
                    dve.wait_ge(w_done, 2 * i + 2)
            kept = 0
            for m in range(2, MARKS):
                mark(m)
                if m == MARKS // 2:
                    split_basis(0)
                while (kept + 1) * CG <= m * MG:
                    keep(kept)
                    kept += 1
            for g in range(kept, GROUPS):
                keep(g)
            dve.wait_ge(same_in[0], 16)

            def split_rows(s, k):
                wait(dve, gt_moved, k + 1)
                wait(dve, based, k * 2 - 2)
                nc.vector.tensor_tensor(gT_lo[:, s, :, :], gT[:, s, :, :], gT_hi[:, s, :, :].bitcast(F32),
                                        ALU.subtract).then_inc(gt_rest, 1)

            def messages(s, k, half, l, sharing):
                wait(dve, based, k * 2 + (1 + half))
                if half == 0:
                    wait(dve, coef_set, k + 1)
                    wait(dve, msg_t, k - 1)
                if sharing:
                    wait(dve, shared, k * 2 + (half + 1 - unshared(l)))
                for b in range(half * NB // 2, (half + 1) * NB // 2 - sharing):
                    for j in range(2):
                        cf = coef_now[:, s, j * NB + b:j * NB + b + 1]
                        o = msg[:, s, j, :]
                        y = ps_b[half][:, j, b % (NB // 2), :]
                        if b == 0:
                            i = nc.vector.tensor_scalar(o, y, cf, None, ALU.mult)
                        else:
                            before = 6 + 2 * j if sharing and b == NB // 2 else 2 * b + j - 1
                            dve.wait_ge(linked, k * 16 + before)
                            i = nc.vector.scalar_tensor_tensor(out=o, in0=y, scalar=cf, in1=o,
                                                               op0=ALU.mult, op1=ALU.add)
                        i.then_inc(linked, 2 if sharing and b % (NB // 2) == NB // 2 - 2 else 1)

            def scan(c, s, k, first):
                wait(dve, msg_t, k + 1)
                wait(dve, run_t, k - 1)
                if not first:
                    wait(dve, scanned, k)
                nc.vector.tensor_tensor_scan(run[:, s, :], same[:, bass.ds(c * P, 2 * P)],
                                             ps_m[:, 0:2, :].rearrange("p j e -> p (j e)"),
                                             0.0 if first else run[:, 1 - s, 2 * P - 1:2 * P],
                                             ALU.mult, ALU.add).then_inc(scanned, 1)

            def slow_chunks(l):
                for b in range(NBUF):
                    dve.wait_ge(y_out[b], y_total(b, l))
                dve.wait_ge(slow_mask, 3 * l + 3)
                nc.vector.tensor_copy(slow_row, slow_row_i).then_inc(slow_v, 1)
                with dve.Fori(0, CH) as c:
                    n = c + l * CH
                    col = dst_f[:, bass.ds(c, 1)]
                    v = n * 4 + (l + 1)
                    dve.wait_ge(slow_v, v)
                    nc.vector.tensor_scalar(col_b, ident[:, :], 0.0, col, ALU.mult, ALU.add).then_inc(slow_col, 1)
                    dve.wait_ge(slow_dst, n + 1)
                    nc.vector.tensor_scalar(joins, ps_x[:, 0:P], col, last_f[:, bass.ds(c, 1)],
                                            ALU.is_equal, ALU.mult).then_inc(slow_join, 1)
                    nc.vector.scalar_tensor_tensor(out=after, in0=ps_x[:, 0:P], scalar=col, in1=later_m,
                                                   op0=ALU.is_equal, op1=ALU.mult).then_inc(slow_v, 1)
                    dve.wait_ge(slow_v, v + 1)
                    nc.vector.reduce_max(later, after, axis=AX.X).then_inc(slow_v, 1)
                    nc.vector.tensor_tensor(away_s, slow_row, col, ALU.subtract).then_inc(slow_v, 1)
                    dve.wait_ge(slow_v, v + 3)
                    dve.wait_ge(slow_put, n * 16)
                    nc.vector.scalar_tensor_tensor(out=slow_put_i, in0=later, scalar=away_s, in1=col,
                                                   op0=ALU.mult, op1=ALU.add).then_inc(slow_v, 1)
                    dve.wait_ge(slow_v, v + 4)
                    dve.wait_ge(slow_sum, n + 1)
                    nc.vector.tensor_copy(whole, ps_y[:, 0:D]).then_inc(slow_ready, 1)

            dve_unsorted = dve.value_load(unsorted_i[0:1, 0:1], min_val=0, max_val=E)

            for l in range(2):
                K = l * PAIRS

                def step_m(it, u, a_, m_, c_, sharing, l=l, K=K):
                    if m_:
                        messages((u + 1) % 2, it * G + (K + u - 1), 0, l, sharing)
                    if a_:
                        split_rows(u % 2, it * G + (K + u))
                    if m_:
                        messages((u + 1) % 2, it * G + (K + u - 1), 1, l, sharing)
                    if c_:
                        scan(it * U + (2 * u - 4), u % 2, it * G + (K + u - 2), isinstance(it, int) and it * G + u == 2)

                if l:
                    split_basis(l)
                for it in range(2):
                    for u in range(G):
                        step_m(it, u, True, it or u, it, False)
                if l == 0:
                    dve.wait_ge(same_in[1], 2 * 16)
                with dve.Fori(2, MIXED[l]) as it:
                    for u in range(G):
                        step_m(it, u, True, True, True, False)
                if l == 0:
                    dve.wait_ge(same_in[2], 3 * 16)
                step_m(MIXED[l], 0, True, True, True, False)
                step_m(MIXED[l], 1, True, True, True, True)
                with dve.Fori(MIXED[l] + 1, TURNS) as it:
                    for u in range(G):
                        step_m(it, u, True, True, True, True)
                step_m(TURNS, 0, False, True, True, True)
                step_m(TURNS, 1, False, False, True, True)
                with dve.If(dve_unsorted > 0):
                    slow_chunks(l)

            dve.wait_ge(x_early, 16 * XBUF)

            def final_sums(turn, j, skip, rows, nj):
                k = turn * FBUF + j
                h = f_rows(j)[0:rows, 0:nj, :].rearrange("p j d -> p (j d)")
                xx = f_x(k - skip)[0:rows, 0:nj, :].rearrange("p j d -> p (j d)")
                if skip:
                    dve.wait_ge(fx_in[j], turn * 16 - 16 * (XTURNS - 1))
                dve.wait_ge(f_bias, k + 1)
                nc.vector.scalar_tensor_tensor(out=h, in0=h, scalar=0.0, in1=xx,
                                               op0=ALU.max, op1=ALU.add).then_inc(f_sum, 1)

            def final_scales(turn, j, step, rows=P, nj=FJ):
                k = turn * FBUF + j
                f = {n: a[0:rows, 0:nj] for n, a in f_small(j).items()}
                if step == 0:
                    dve.wait_ge(f_stat, k + 1)
                    nc.vector.tensor_tensor(f["d"], f["bn"][:, :, 1], f["bn"][:, :, 4], ALU.subtract)
                    nc.vector.tensor_tensor(f["q"], f["bn"][:, :, 2], f["bn"][:, :, 5], ALU.add)
                    nc.vector.tensor_tensor(f["s"], f["bn"][:, :, 1], f["bn"][:, :, 4], ALU.add).then_inc(f_var, 1)
                elif step == 1:
                    dve.wait_ge(f_var, k * 4 + 1)
                    nc.vector.tensor_tensor(f["d"], f["d"], f["d"], ALU.mult)
                    nc.vector.tensor_scalar(f["q"], f["q"], 1.0 / D, EPS, ALU.mult, ALU.add).then_inc(f_var, 1)
                elif step == 2:
                    dve.wait_ge(f_var, k * 4 + 2)
                    nc.vector.scalar_tensor_tensor(out=f["v"], in0=f["d"], scalar=0.25, in1=f["q"],
                                                   op0=ALU.mult, op1=ALU.add).then_inc(f_var, 1)
                elif step == 3:
                    dve.wait_ge(f_std, k + 1)
                    nc.vector.reciprocal(f["r"], f["q"]).then_inc(f_var, 1)
                else:
                    dve.wait_ge(f_var, k * 4 + 4)
                    nc.vector.scalar_tensor_tensor(out=f["o"], in0=f["s"], scalar=-0.5, in1=f["r"],
                                                   op0=ALU.mult, op1=ALU.mult).then_inc(f_norm, 1)

            def final_block(turn, j, skip, rows=P, nj=FJ, before=True):
                k = turn * FBUF + j
                final_sums(turn, j, skip, rows, nj)
                if before:
                    final_scales(turn, j - 1, 0)
                dve.wait_ge(f_sum, k + 1)
                for i in range(FJ):
                    if i < nj:
                        ins = nc.vector.bn_stats(f_small(j)["bn"][0:rows, i, :], f_rows(j)[0:rows, i, :])
                        if i == nj - 1:
                            ins.then_inc(f_stat, 1)
                    if before and i in (1, 3, 8, 9):
                        final_scales(turn, j - 1, (1, 3, 8, 9).index(i) + 1)

            for j in range(FBUF):
                final_block(0, j, 0, before=j > 0)
            with dve.Fori(1, XTURNS) as t:
                for j in range(FBUF):
                    final_block(t, j, 0)
            with dve.Fori(XTURNS, FTURNS) as t:
                for j in range(FBUF):
                    final_block(t, j, XBUF)
            for j in range(FN % FBUF):
                final_block(FTURNS, j, XBUF)
            final_block(FTURNS, FN % FBUF, XBUF, FTAIL, 1)
            for step in range(5):
                final_scales(FTURNS, FN % FBUF, step, FTAIL, 1)

        @block.scalar
        def _(act):
            def stage_rows(p, u, k, turn16):
                for j in range(2):
                    wait(act, gathered[(2 * u + j) % U], turn16)
                wait(act, gt_made, k)
                nc.scalar.copy(stage[:, :, :], sums[:, bass.ds(p * 2, 2), :]).then_inc(staged, 1)

            def set_coef(l, p, s, k):
                wait(act, linked, k * 16 - 16)
                nc.scalar.copy(coef_now[:, s, :].rearrange("p (a b) -> p a b", a=2),
                               coef[l][:, bass.ds(p * 2, 2), :]).then_inc(coef_set, 1)

            def move_t(l, o, i):
                if l == 0:
                    return nc.scalar.copy(o, i)
                return nc.scalar.activation(o, i, ACT.Relu, bias=bias1_c[:, 0:1])

            def move_run(p, k):
                wait(act, run_t, k + 1)
                nc.scalar.copy(sums[:, bass.ds(p * 2, 2), :], ps_g[:, 2:4, :]).then_inc(summed, 1)

            def move_x(l, h, s, cols=Q * P):
                wait(act, xt_made, h + 1)
                wait(act, y_made, h - 1)
                move_t(l, xT[:, s, 0:cols], ps_x[:, 0:cols]).then_inc(xt_moved, 1)

            def move_y(h, b, j, nj=Q, tail=0):
                wait(act, y_made, h + 1)
                i = nc.scalar.copy(yout[:, b, j:j + nj, :].rearrange("p j d -> p (j d)"), ps_y[:, 0:nj * D])
                if tail:
                    i = nc.scalar.copy(yout[0:tail, b, j + nj, :], ps_y[0:tail, nj * D:(nj + 1) * D])
                i.then_inc(y_moved, 1)

            def split_basis(l):
                act.wait_ge(basis_in, 16 * (l + 1))
                nc.scalar.copy(basis_hi[:, :], basis_raw.rearrange("p b d -> p (b d)")).then_inc(basis_top, 1)

            for l in range(2):
                K = l * PAIRS
                H = l * HALVES
                if l:
                    act.wait_ge(weights_in, 16 * 3)

                def dense_1(t, u, l=l, H=H):
                    h = t * (2 * G) + (H + 2 * u)
                    move_x(l, h, 0)
                    if not (isinstance(t, int) and t == 0 and u == 0):
                        move_y(h - 1, (u + 1) % 2, Q)

                def dense_2(t, u, l=l, H=H):
                    h = t * (2 * G) + (H + 2 * u)
                    move_x(l, h + 1, 1)
                    wait(act, y_out[u], t * 16 + (y_total(u, 0) if l else 0))
                    move_y(h, u % 2, 0)

                def step_m(it, u, next_, a_, d_, dense, sharing=False, l=l, K=K, H=H):
                    p = it * G + u
                    k = it * G + (K + u)
                    if sharing:
                        make_shares((u + 1) % 2, k - 1, 0)
                    if a_:
                        wait(act, gt_made, k + 1)
                        if d_:
                            wait(act, run_t, k - (LAG - 1))
                        wait(act, based, k * 2 - 2)
                        wait(act, gt_rest, k - 1)
                        move_t(l, gT[:, u % 2, :, :], ps_g[:, 0:2, :])
                        move_t(l, gT_hi[:, u % 2, :, :], ps_g[:, 0:2, :]).then_inc(gt_moved, 1)
                    if d_:
                        move_run(it * G + (u - LAG), k - LAG)
                    if sharing:
                        make_shares((u + 1) % 2, k - 1, 1)
                    if a_:
                        set_coef(l, p, u % 2, k)
                    if dense:
                        dense_1(it + DFIRST[l], u)
                    if next_:
                        it_ = it if u + 1 < G else it + 1
                        stage_rows(it * G + (u + 1), (u + 1) % G, k + 1, it_ * 16 + (16 + 16 * l * TURNS))
                    if dense:
                        dense_2(it + DFIRST[l], u)

                def make_shares(s, k, half):
                    wait(act, based, k * 2 + (1 + half))
                    if half == 0:
                        wait(act, coef_set, k + 1)
                        wait(act, msg_t, k - 1)
                    b = (half + 1) * NB // 2 - 1
                    for j in range(2):
                        i = nc.scalar.activation(share[:, s, half, j, :], ps_b[half][:, j, NB // 2 - 1, :], ACT.Copy,
                                                 scale=coef_now[:, s, j * NB + b:j * NB + b + 1])
                    i.then_inc(shared, 1)

                if l:
                    act.wait_ge(based, 2 * PAIRS)
                    split_basis(l)
                def dense_turn(t):
                    for u in range(G):
                        dense_1(t, u)
                        dense_2(t, u)

                if l == 0:
                    dense_turn(0)
                    act.dma_start(basis_raw, basis1.rearrange("b i o -> i b o")).then_inc(basis_in, 16)
                    act.dma_start(loop_w[1][:, :], loop_w2).then_inc(weights_in, 16)
                    act.dma_start(bias1_c[:, :], bias1.rearrange("(p a) -> p a", a=1)).then_inc(weights_in, 16)
                    act.dma_start(bias2_b[:, :], bias2.partition_broadcast(P)).then_inc(weights_in, 16)
                    dense_turn(1)
                    split_basis(l)
                    with act.Fori(2, DFIRST[0]) as t:
                        dense_turn(t)
                stage_rows(0, 0, K, 16 + 16 * l * TURNS)
                if l == 0:
                    for n in range(2):
                        act.dma_start(nodes[n][DUMMY:ROWS, :].rearrange("(s p) d -> p s d", p=P), zeros[:, :, :]).then_inc(zero_w, 16)
                    act.wait_ge(coef_ok, 1)
                for it in range(2):
                    for u in range(G):
                        step_m(it, u, True, True, False, True)
                if l == 0:
                    act.wait_ge(coef_ok, GROUPS)
                with act.Fori(2, MIXED[l]) as it:
                    for u in range(G):
                        step_m(it, u, True, True, True, True)
                h = H + 2 * NBLK
                move_x(l, h, 0)
                move_y(h - 1, 1, Q)
                move_x(l, h + 1, 1, (TAILQ - Q) * P + TAIL)
                act.wait_ge(y_out[0], y_total(0, l) - 32)
                move_y(h, 0, 0)
                move_y(h + 1, 0, Q, TAILQ - Q, TAIL)
                step_m(MIXED[l], 0, True, True, True, False)
                act.wait_ge(y_out[1], y_total(1, l))
                step_m(MIXED[l], 1, True, True, True, False, True)
                with act.Fori(MIXED[l] + 1, TURNS - 1) as it:
                    for u in range(G):
                        step_m(it, u, True, True, True, False, True)
                for u in range(G):
                    step_m(TURNS - 1, u, u < G - 1, True, True, False, True)
                for m in range(LAG):
                    step_m(TURNS + m // G, m % G, False, False, True, False, m < 1)

            def std(turn, j, rows=P, nj=FJ):
                f = f_small(j)
                act.wait_ge(f_var, (turn * FBUF + j) * 4 + 3)
                nc.scalar.activation(f["q"][0:rows, 0:nj], f["v"][0:rows, 0:nj], ACT.Sqrt).then_inc(f_std, 1)

            def normalise(turn, j, skip, i0, i1, rows=P, nj=FJ):
                f = f_small(j)
                if i0 == 0:
                    act.wait_ge(f_norm, turn * FBUF + (j + 1))
                xx = f_x(turn * FBUF + (j - skip))
                for i in range(i0, i1):
                    ins = nc.scalar.activation(xx[0:rows, i, :], f_rows(j)[0:rows, i, :], ACT.Identity,
                                               bias=f["o"][0:rows, i:i + 1], scale=f["r"][0:rows, i:i + 1])
                if i1 == nj:
                    ins.then_inc(f_done, 1)

            def final_block(turn, j, skip, before=True):
                if before:
                    normalise(turn, j - 2, skip, 0, FJ - 3)
                std(turn, j - 1)
                if before:
                    normalise(turn, j - 2, skip, FJ - 3, FJ)

            for j in range(1, FBUF):
                final_block(0, j, 0, j > 1)
            with act.Fori(1, XTURNS) as t:
                for j in range(FBUF):
                    final_block(t, j, 0)
            for j in range(2):
                final_block(XTURNS, j, 0)
            for j in range(2, FBUF):
                final_block(XTURNS, j, XBUF)
            with act.Fori(XTURNS + 1, FTURNS) as t:
                for j in range(FBUF):
                    final_block(t, j, XBUF)
            for j in range(FN % FBUF + 1):
                final_block(FTURNS, j, XBUF)
            last = FN % FBUF
            normalise(FTURNS, last - 1, XBUF, 0, FJ)
            std(FTURNS, last, FTAIL, 1)
            normalise(FTURNS, last, XBUF, 0, 1, FTAIL, 1)

        @block.tensor
        def _(pe):
            def node_t(h, b, j, tiles=Q, tail=0, x_count=None):
                if x_count is not None:
                    pe.wait_ge(x_in[b], x_count)
                wait(pe, xt_moved, h)
                for q in range(tiles):
                    i = nc.tensor.transpose(ps_x[:, q * P:(q + 1) * P], xin[:, b, j + q, :], ident[:, :])
                if tail:
                    i = nc.tensor.transpose(ps_x[:, tiles * P:tiles * P + tail], xin[0:tail, b, j + tiles, :],
                                            ident[0:tail, 0:tail])
                i.then_inc(xt_made, 1)

            def node_mm(l, h, s, tiles=Q, tail=0):
                wait(pe, xt_moved, h + 1)
                wait(pe, y_moved, h)
                for q in range(tiles):
                    i = nc.tensor.matmul(ps_y[:, q * D:(q + 1) * D], xT[:, s, q * P:(q + 1) * P],
                                         loop_w[l][:, :], start=True, stop=True)
                if tail:
                    i = nc.tensor.matmul(ps_y[0:tail, tiles * D:(tiles + 1) * D],
                                         xT[:, s, tiles * P:tiles * P + tail],
                                         loop_w[l][:, :], start=True, stop=True)
                i.then_inc(y_made, 1)

            def dense_1(l, t, u):
                h = t * (2 * G) + (l * HALVES + 2 * u)
                node_t(h, u, 0, x_count=t * 16 + (16 + (y_total(u, 0) if l else 0)))
                if not (isinstance(t, int) and t == 0 and u == 0):
                    node_mm(l, h - 1, 1)

            def dense_2(l, t, u):
                h = t * (2 * G) + (l * HALVES + 2 * u)
                node_t(h + 1, u, Q)
                node_mm(l, h, 0)

            def dense_turn(l, t):
                for u in range(G):
                    dense_1(l, t, u)
                    dense_2(l, t, u)

            pe.wait_ge(ident_ok, 2)
            pe.wait_ge(loop_in, 16)
            dense_turn(0, 0)
            pe.wait_ge(vdone, 11)
            homes = {"src": (0, 0), "dst": (0, 1), "last": (1, 0)}
            for k, (s, a) in homes.items():
                o = ps_b[s][:, a, :, :].rearrange("p a d -> p (a d)")
                nc.tensor.transpose(o[:, 0:P], val[k][:, 0, :], ident[:, :])
                nc.tensor.transpose(o[:, P:CH], val[k][0:CH - P, 1, :], ident[0:CH - P, 0:CH - P])
            nc.tensor.matmul(ps_m[0:1, 0, 0:1], ones_c, worst, start=True, stop=True).then_inc(setup_t, 1)
            def make_coefficients(g):
                pe.wait_ge(onehot, -(-min((g + 1) * CG, CH) // MG))
                if g >= 4:
                    pe.wait_ge(coef_ok, g - 3)
                for c in range(g * CG, min((g + 1) * CG, CH)):
                    i = (c - g * CG) * PARTS * 2 * NB
                    ins = nc.tensor.matmul(coef_bank(g)[:, i:i + PARTS * 2 * NB], rel_b[:, c * P:(c + 1) * P],
                                           w_parts[:, :, :].rearrange("r i b -> r (i b)"), start=True, stop=True)
                ins.then_inc(coef_made, 1)

            dense_turn(0, 1)
            pe.wait_ge(w_done, 2 * PARTS - 1)
            pe.wait_ge(idx_ok, 1)
            blocks = [(t, u) for t in range(2, DFIRST[0]) for u in range(G)]
            for n, (t, u) in enumerate(blocks):
                for g in range(n * GROUPS // len(blocks), (n + 1) * GROUPS // len(blocks)):
                    make_coefficients(g)
                dense_1(0, t, u)
                dense_2(0, t, u)
            pe_unsorted = pe.value_load(unsorted_i[0:1, 0:1], min_val=0, max_val=E)

            def slow_chunks(l):
                pe.wait_ge(summed, PAIRS * (l + 1))
                with pe.Fori(0, CH) as c:
                    pe.wait_ge(slow_col, c + (l * CH + 1))
                    nc.tensor.matmul(ps_x[:, 0:P], col_b, ident[:, :], start=True, stop=True).then_inc(slow_dst, 1)
                    pe.wait_ge(slow_join, c + (l * CH + 1))
                    nc.tensor.matmul(ps_y[:, 0:D], joins, sums[:, bass.ds(c, 1), :].rearrange("p a d -> p (a d)"),
                                     start=True, stop=True).then_inc(slow_sum, 1)

            for l in range(2):
                K = l * PAIRS
                H = l * HALVES

                def times_bases(k, s, half):
                    wait(pe, gt_moved, k + 1)
                    wait(pe, linked, k * 16 - (8 if half == 0 else 0))
                    w = NB // 2 * D
                    hi = basis_hi[:, half * w:(half + 1) * w]
                    lo = basis_lo[:, half * w:(half + 1) * w]
                    o = [ps_b[half][:, j, :, :].rearrange("p b d -> p (b d)") for j in range(2)]
                    for j in range(2):
                        nc.tensor.matmul(o[j], gT_hi[:, s, j, :], hi, start=True, stop=False)
                        nc.tensor.matmul(o[j], gT_hi[:, s, j, :], lo, start=False, stop=False)
                    wait(pe, gt_rest, k + 1)
                    for j in range(2):
                        i = nc.tensor.matmul(o[j], gT_lo[:, s, j, :], hi, start=False, stop=True)
                    i.then_inc(based, 1)

                def step_m(it, u, a_, b_, c_, d_, dense, sharing=False, l=l, K=K, H=H):
                    k = it * G + (K + u)
                    s = u % 2
                    if b_:
                        wait(pe, gt_moved, k)
                        times_bases(k - 1, 1 - s, 0)
                    wait(pe, gt_moved, k if a_ or b_ else K + PAIRS)
                    wait(pe, summed, k - LAG if d_ else (K if l else 0))
                    if a_:
                        wait(pe, staged, k + 1)
                        for j in range(2):
                            i = nc.tensor.transpose(ps_g[:, j, :], stage[:, j, :], ident[:, :])
                        i.then_inc(gt_made, 1)
                    if d_:
                        wait(pe, scanned, k - (LAG - 1))
                        for j in range(2):
                            i = nc.tensor.transpose(ps_g[:, 2 + j, :], run[:, s, j * P:(j + 1) * P], ident[:, :])
                        i.then_inc(run_t, 1)
                    if dense:
                        dense_1(l, it + DFIRST[l], u)
                    if b_:
                        times_bases(k - 1, 1 - s, 1)
                    if c_:
                        wait(pe, linked, k * 16 - 16)
                        wait(pe, scanned, k - 2)
                        for j in range(2):
                            if sharing:
                                nc.tensor.matmul(ps_m[:, j, :], msg[:, s, j, :], ident[:, :], start=True, stop=False)
                                nc.tensor.matmul(ps_m[:, j, :], share[:, s, 0, j, :], ident[:, :],
                                                 start=False, stop=False)
                                i = nc.tensor.matmul(ps_m[:, j, :], share[:, s, 1, j, :], ident[:, :],
                                                     start=False, stop=True)
                            else:
                                i = nc.tensor.transpose(ps_m[:, j, :], msg[:, s, j, :], ident[:, :])
                        i.then_inc(msg_t, 1)
                    if dense:
                        dense_2(l, it + DFIRST[l], u)

                if l:
                    pe.wait_ge(weights_in, 16 * 3)
                else:
                    pe.wait_ge(coef_ok, GROUPS)
                pe.wait_ge(basis_ok, l + 1)
                for it in range(2):
                    for u in range(G):
                        step_m(it, u, True, it or u, it, False, True)
                with pe.Fori(2, MIXED[l]) as it:
                    for u in range(G):
                        step_m(it, u, True, True, True, True, True)
                h = H + 2 * NBLK
                node_t(h, 0, 0, x_count=y_total(0, l))
                node_mm(l, h - 1, 1)
                node_t(h + 1, 0, Q, TAILQ - Q, TAIL)
                node_mm(l, h, 0)
                node_mm(l, h + 1, 1, TAILQ - Q, TAIL)
                for u in range(G):
                    step_m(MIXED[l], u, True, True, True, True, False)
                with pe.Fori(MIXED[l] + 1, TURNS) as it:
                    for u in range(G):
                        step_m(it, u, True, True, True, True, False, True)
                for m in range(LAG):
                    step_m(TURNS + m // G, m % G, False, m < 1, m < 2, True, False, True)
                with pe.If(pe_unsorted > 0):
                    slow_chunks(l)


_INS = ['x', 'src', 'dst', 'edge_type_16', 'L0_gnn_basis1', 'L0_gnn_w_comp1', 'L0_gnn_loop_w1', 'L0_gnn_bias1',
        'L0_gnn_basis2', 'L0_gnn_w_comp2', 'L0_gnn_loop_w2', 'L0_gnn_bias2']


def kernel(**inputs):
    import numpy as _np
    import concourse.bacc as _bacc
    from concourse import mybir as _mybir
    from concourse.bass_utils import run_bass_kernel_spmd as _run

    nc = _bacc.Bacc("TRN2", target_bir_lowering=False, num_devices=1)
    arrays, args = {}, []
    for name in _INS:
        a = _np.ascontiguousarray(inputs[name])
        arrays[f"in_{name}"] = a
        args.append(nc.dram_tensor(f"in_{name}", a.shape, _mybir.dt.from_np(a.dtype), kind="ExternalInput").ap())
    args.append(nc.dram_tensor("out_rows", (N, D), _mybir.dt.float32, kind="ExternalOutput").ap())
    build_rgcn(nc, *args)
    r = _run(nc, [arrays], core_ids=[0])
    return r.results[0]["out_rows"]
```
